# Optimizing a Trainium2 kernel written in Bass

```python
import numpy as np
import jax
import jax.numpy as jnp

def _softmax(x, axis=-1):
    return jax.nn.softmax(x, axis=axis)

def _gelu(x):
    return jax.nn.gelu(x, approximate=True)

def _silu(x):
    return jax.nn.silu(x)

def _sigmoid(x):
    return jax.nn.sigmoid(x)

def _layernorm(x, axis=-1, eps=1e-05):
    m = jnp.mean(x, axis=axis, keepdims=True)
    v = jnp.var(x, axis=axis, keepdims=True)
    return (x - m) / jnp.sqrt(v + eps)

def _scatter_add(tgt, idx, src, axis=0):
    return tgt.at[idx].add(src)

def _segment_sum(src, seg, n):
    return jax.ops.segment_sum(src, seg, n)
kernel_name = 'mk_flamingo_gated_d1_seqx_r8_3f3221'

def setup_inputs(seed: int=0):
    np.random.seed(seed)
    _w = jnp.asarray

    def _rec_inputs():
        import jax
        import jax.numpy as jnp
        _rk = jax.random.key(seed)
        x = -4.161e-06 + 1 * jax.random.normal(jax.random.fold_in(_rk, 1), (8, 256, 256), jnp.float32)
        _lenS = 256 - jax.random.randint(jax.random.fold_in(_rk, 7), (8,), 0, max(1, 256 // 4) + 1, jnp.int32)
        _lenS2 = 1601 - jax.random.randint(jax.random.fold_in(_rk, 8), (8,), 0, max(1, 1601 // 4) + 1, jnp.int32)
        _ctx_2048P = jax.random.normal(jax.random.fold_in(_rk, 11), (8, 16, 256), jnp.float32)
        _ctx_2048c = jax.random.dirichlet(jax.random.fold_in(_rk, 511), 0.3 * jnp.ones((16,), jnp.float32), (8, 1601))
        _ctx_2048t = jnp.einsum('bsk,bkd->bsd', _ctx_2048c, _ctx_2048P)
        _ctx_2048t = _ctx_2048t * jax.lax.rsqrt(jnp.mean(jnp.square(_ctx_2048t)) + 1e-12) * 0.953939
        ctx_2048 = -0.000192764 + 0.999654 * (_ctx_2048t + 0.3 * jax.random.normal(jax.random.fold_in(_rk, 611), (8, 1601, 256), jnp.float32))
        _g = jax.random.normal(jax.random.fold_in(_rk, 9001), (2, 1), jnp.float32)
        _g = jnp.sign(_g) * jnp.maximum(jnp.abs(_g), 1.0) + (_g == 0) * 1.0
        g_xattn = _g[0]
        g_ffn = _g[1]
        return (x, ctx_2048, g_xattn, g_ffn)
    x, ctx_2048, g_xattn, g_ffn = _rec_inputs()

    def _L0_xattn_setup():
        import jax, jax.numpy as jnp
        import numpy as np
        FP8_MAX = 448.0
        EPS = 1e-05

        def _fp8_roundtrip(x):
            return x.astype(jnp.float8_e4m3fn).astype(jnp.float32)

        def _div_clamp_fp8(x, scale):
            y = jnp.clip(x.astype(jnp.float32) / scale, -FP8_MAX, FP8_MAX)
            y = y.astype(jnp.bfloat16).astype(jnp.float32)
            return _fp8_roundtrip(y)

        def _ln(x, w, b):
            mu = jnp.mean(x, axis=-1, keepdims=True)
            var = jnp.mean(jnp.square(x - mu), axis=-1, keepdims=True)
            return (x - mu) * jax.lax.rsqrt(var + EPS) * w + b

        def _fp8_linear_pertensor(x, wq, w_scale, in_scale):
            xq = _div_clamp_fp8(x, in_scale)
            return jnp.einsum('bsi,oi->bso', xq * in_scale, wq) * w_scale

        def _gqa(q, k, v):
            scale = 1.0 / np.sqrt(q.shape[-1])
            scores = jnp.einsum('bsghd,btgd->bghst', q, k) * scale
            p = jax.nn.softmax(scores, axis=-1)
            return jnp.einsum('bghst,btgd->bsghd', p, v)
        key = jax.random.key(seed)
        ks = jax.random.split(key, 8)
        B, S, SC, H, NH, G, D = (2, 256, 64, 256, 16, 8, 128)

        def qw(k, out_f, in_f):
            w = jax.random.normal(k, (out_f, in_f), jnp.float32) * 0.02
            sc = jnp.max(jnp.abs(w)) / FP8_MAX
            return (_fp8_roundtrip(w / sc), sc.astype(jnp.float32))
        wq, wq_s = qw(ks[0], NH * D, H)
        wqx, wqx_s = qw(ks[1], NH * D, H)
        wk, wk_s = qw(ks[2], G * D, H)
        wv, wv_s = qw(ks[3], G * D, H)
        wproj, wp_s = qw(ks[4], H, 2 * NH * D)
        return {'hidden_states': jax.random.normal(ks[5], (B, S, H), jnp.float32), 'cond': jax.random.normal(ks[6], (B, SC, H), jnp.float32), 'ln_w': jnp.ones((H,), jnp.float32), 'ln_b': jnp.zeros((H,), jnp.float32), 'wq': wq, 'wq_scale': wq_s, 'q_in_scale': jnp.full((H,), 0.05, jnp.float32), 'wqx': wqx, 'wqx_scale': wqx_s, 'qx_in_scale': jnp.full((H,), 0.05, jnp.float32), 'wk': wk, 'wk_scale': wk_s, 'k_in_scale': jnp.full((H,), 0.05, jnp.float32), 'wv': wv, 'wv_scale': wv_s, 'v_in_scale': jnp.full((H,), 0.05, jnp.float32), 'w_kv_x': jax.random.normal(ks[7], (2 * G * D, H), jnp.float32) * 0.02, 'qln_w': jnp.ones((D,), jnp.float32), 'qln_b': jnp.zeros((D,), jnp.float32), 'kln_w': jnp.ones((D,), jnp.float32), 'kln_b': jnp.zeros((D,), jnp.float32), 'qxln_w': jnp.ones((D,), jnp.float32), 'qxln_b': jnp.zeros((D,), jnp.float32), 'kxln_w': jnp.ones((D,), jnp.float32), 'kxln_b': jnp.zeros((D,), jnp.float32), 'wproj': wproj, 'proj_w_scale': wp_s, 'proj_in_scale': jnp.asarray(0.05, jnp.float32), 'proj_smooth': jnp.full((2 * NH * D,), 0.05, jnp.float32)}
    _L0_xattn_all = _L0_xattn_setup()
    _L0_xattn_in = {k: v for k, v in _L0_xattn_all.items() if k in ('ln_w', 'ln_b', 'wq', 'wq_scale', 'q_in_scale', 'wqx', 'wqx_scale', 'qx_in_scale', 'wk', 'wk_scale', 'k_in_scale', 'wv', 'wv_scale', 'v_in_scale', 'w_kv_x', 'qln_w', 'qln_b', 'kln_w', 'kln_b', 'qxln_w', 'qxln_b', 'kxln_w', 'kxln_b', 'wproj', 'proj_w_scale', 'proj_in_scale', 'proj_smooth')}
    del _L0_xattn_all

    def _L0_ffn_setup():
        import jax, jax.numpy as jnp
        import numpy as np
        E, H, I = (8, 256, 512)
        TOP_K = 1
        B, S = (1, 256)
        key = jax.random.key(seed)
        ks = jax.random.split(key, 7)
        std = 0.02
        return {'hidden_states': jax.random.normal(ks[0], (B, S, H), dtype=jnp.float32), 'router_w': jax.random.normal(ks[1], (E, H), dtype=jnp.float32) * std, 'gate_up_proj': jax.random.normal(ks[2], (E, H, 2 * I), dtype=jnp.float32) * std, 'down_proj': jax.random.normal(ks[3], (E, I, H), dtype=jnp.float32) * std, 'shared_gate_w': jax.random.normal(ks[4], (H, I), dtype=jnp.float32) * std, 'shared_up_w': jax.random.normal(ks[5], (H, I), dtype=jnp.float32) * std, 'shared_down_w': jax.random.normal(ks[6], (I, H), dtype=jnp.float32) * std}
    _L0_ffn_all = _L0_ffn_setup()
    _L0_ffn_in = {k: v for k, v in _L0_ffn_all.items() if k in ('router_w', 'gate_up_proj', 'down_proj', 'shared_gate_w', 'shared_up_w', 'shared_down_w')}
    del _L0_ffn_all
    return {'x': x, 'ctx_2048': ctx_2048, 'g_xattn': g_xattn, 'g_ffn': g_ffn, 'L0_xattn_ln_w': _L0_xattn_in['ln_w'], 'L0_xattn_ln_b': _L0_xattn_in['ln_b'], 'L0_xattn_wq': _L0_xattn_in['wq'], 'L0_xattn_wq_scale': _L0_xattn_in['wq_scale'], 'L0_xattn_q_in_scale': _L0_xattn_in['q_in_scale'], 'L0_xattn_wqx': _L0_xattn_in['wqx'], 'L0_xattn_wqx_scale': _L0_xattn_in['wqx_scale'], 'L0_xattn_qx_in_scale': _L0_xattn_in['qx_in_scale'], 'L0_xattn_wk': _L0_xattn_in['wk'], 'L0_xattn_wk_scale': _L0_xattn_in['wk_scale'], 'L0_xattn_k_in_scale': _L0_xattn_in['k_in_scale'], 'L0_xattn_wv': _L0_xattn_in['wv'], 'L0_xattn_wv_scale': _L0_xattn_in['wv_scale'], 'L0_xattn_v_in_scale': _L0_xattn_in['v_in_scale'], 'L0_xattn_w_kv_x': _L0_xattn_in['w_kv_x'], 'L0_xattn_qln_w': _L0_xattn_in['qln_w'], 'L0_xattn_qln_b': _L0_xattn_in['qln_b'], 'L0_xattn_kln_w': _L0_xattn_in['kln_w'], 'L0_xattn_kln_b': _L0_xattn_in['kln_b'], 'L0_xattn_qxln_w': _L0_xattn_in['qxln_w'], 'L0_xattn_qxln_b': _L0_xattn_in['qxln_b'], 'L0_xattn_kxln_w': _L0_xattn_in['kxln_w'], 'L0_xattn_kxln_b': _L0_xattn_in['kxln_b'], 'L0_xattn_wproj': _L0_xattn_in['wproj'], 'L0_xattn_proj_w_scale': _L0_xattn_in['proj_w_scale'], 'L0_xattn_proj_in_scale': _L0_xattn_in['proj_in_scale'], 'L0_xattn_proj_smooth': _L0_xattn_in['proj_smooth'], 'L0_ffn_router_w': _L0_ffn_in['router_w'], 'L0_ffn_gate_up_proj': _L0_ffn_in['gate_up_proj'], 'L0_ffn_down_proj': _L0_ffn_in['down_proj'], 'L0_ffn_shared_gate_w': _L0_ffn_in['shared_gate_w'], 'L0_ffn_shared_up_w': _L0_ffn_in['shared_up_w'], 'L0_ffn_shared_down_w': _L0_ffn_in['shared_down_w']}

def reference(x, ctx_2048, g_xattn, g_ffn, L0_xattn_ln_w, L0_xattn_ln_b, L0_xattn_wq, L0_xattn_wq_scale, L0_xattn_q_in_scale, L0_xattn_wqx, L0_xattn_wqx_scale, L0_xattn_qx_in_scale, L0_xattn_wk, L0_xattn_wk_scale, L0_xattn_k_in_scale, L0_xattn_wv, L0_xattn_wv_scale, L0_xattn_v_in_scale, L0_xattn_w_kv_x, L0_xattn_qln_w, L0_xattn_qln_b, L0_xattn_kln_w, L0_xattn_kln_b, L0_xattn_qxln_w, L0_xattn_qxln_b, L0_xattn_kxln_w, L0_xattn_kxln_b, L0_xattn_wproj, L0_xattn_proj_w_scale, L0_xattn_proj_in_scale, L0_xattn_proj_smooth, L0_ffn_router_w, L0_ffn_gate_up_proj, L0_ffn_down_proj, L0_ffn_shared_gate_w, L0_ffn_shared_up_w, L0_ffn_shared_down_w):
    import jax
    import jax.numpy as jnp

    def _L0_xattn_ref(hidden_states, cond, ln_w, ln_b, wq, wq_scale, q_in_scale, wqx, wqx_scale, qx_in_scale, wk, wk_scale, k_in_scale, wv, wv_scale, v_in_scale, w_kv_x, qln_w, qln_b, kln_w, kln_b, qxln_w, qxln_b, kxln_w, kxln_b, wproj, proj_w_scale, proj_in_scale, proj_smooth):
        import jax, jax.numpy as jnp
        import numpy as np
        FP8_MAX = 448.0
        EPS = 1e-05

        def _fp8_roundtrip(x):
            return x.astype(jnp.float8_e4m3fn).astype(jnp.float32)

        def _div_clamp_fp8(x, scale):
            y = jnp.clip(x.astype(jnp.float32) / scale, -FP8_MAX, FP8_MAX)
            y = y.astype(jnp.bfloat16).astype(jnp.float32)
            return _fp8_roundtrip(y)

        def _ln(x, w, b):
            mu = jnp.mean(x, axis=-1, keepdims=True)
            var = jnp.mean(jnp.square(x - mu), axis=-1, keepdims=True)
            return (x - mu) * jax.lax.rsqrt(var + EPS) * w + b

        def _fp8_linear_pertensor(x, wq, w_scale, in_scale):
            xq = _div_clamp_fp8(x, in_scale)
            return jnp.einsum('bsi,oi->bso', xq * in_scale, wq) * w_scale

        def _gqa(q, k, v):
            scale = 1.0 / np.sqrt(q.shape[-1])
            scores = jnp.einsum('bsghd,btgd->bghst', q, k) * scale
            p = jax.nn.softmax(scores, axis=-1)
            return jnp.einsum('bghst,btgd->bsghd', p, v)
        b, s, _ = hidden_states.shape
        sc = cond.shape[1]
        d = qln_w.shape[0]
        nh = wq.shape[0] // d
        g = wk.shape[0] // d
        hpg = nh // g
        ln_out = _ln(hidden_states, ln_w, ln_b)
        q = _fp8_linear_pertensor(ln_out, wq, wq_scale, q_in_scale).reshape(b, s, g, hpg, d)
        q = _ln(q, qln_w, qln_b)
        k = _fp8_linear_pertensor(ln_out, wk, wk_scale, k_in_scale).reshape(b, s, g, d)
        k = _ln(k, kln_w, kln_b)
        v = _fp8_linear_pertensor(ln_out, wv, wv_scale, v_in_scale).reshape(b, s, g, d)
        core = _gqa(q, k, v).reshape(b, s, nh * d)
        qx = _fp8_linear_pertensor(ln_out, wqx, wqx_scale, qx_in_scale).reshape(b, s, g, hpg, d)
        qx = _ln(qx, qxln_w, qxln_b)
        kvx = jnp.einsum('bsi,oi->bso', cond, w_kv_x)
        kx, vx = jnp.split(kvx, 2, axis=-1)
        kx = _ln(kx.reshape(b, sc, g, d), kxln_w, kxln_b)
        vx = vx.reshape(b, sc, g, d)
        xout = _gqa(qx, kx, vx).reshape(b, s, nh * d)
        cat = jnp.concatenate([core, xout], axis=-1)
        catq = _div_clamp_fp8(cat, proj_smooth)
        return jnp.einsum('bsi,oi->bso', catq, wproj) * (proj_in_scale * proj_w_scale)

    def _L0_ffn_ref(hidden_states, router_w, gate_up_proj, down_proj, shared_gate_w, shared_up_w, shared_down_w):
        import jax, jax.numpy as jnp
        import numpy as np
        E, H, I = (8, 256, 512)
        TOP_K = 1
        B, S = (1, 256)
        orig_shape = hidden_states.shape
        x = hidden_states.reshape(-1, H)
        T = x.shape[0]
        logits = x @ router_w.T
        top_vals, top_idx = jax.lax.top_k(logits, TOP_K)
        scores = jnp.full_like(logits, -jnp.inf)
        scores = scores.at[jnp.arange(T)[:, None], top_idx].set(top_vals)
        scores = jax.nn.sigmoid(scores.astype(jnp.float32)).astype(logits.dtype)
        xr = x[None, :, :] * scores.T[:, :, None]
        gate_up = jnp.einsum('eth,ehf->etf', xr, gate_up_proj)
        gate, up = jnp.split(gate_up, 2, axis=-1)
        routed = jnp.einsum('etf,efh->eth', up * jax.nn.silu(gate), down_proj)
        routed_sum = routed.sum(axis=0)
        shared = jax.nn.silu(x @ shared_gate_w) * (x @ shared_up_w) @ shared_down_w
        return (shared + routed_sum).reshape(orig_shape)
    x = x + jnp.tanh(g_xattn[0]) * _L0_xattn_ref(_layernorm(x, axis=-1), ctx_2048, L0_xattn_ln_w, L0_xattn_ln_b, L0_xattn_wq, L0_xattn_wq_scale, L0_xattn_q_in_scale, L0_xattn_wqx, L0_xattn_wqx_scale, L0_xattn_qx_in_scale, L0_xattn_wk, L0_xattn_wk_scale, L0_xattn_k_in_scale, L0_xattn_wv, L0_xattn_wv_scale, L0_xattn_v_in_scale, L0_xattn_w_kv_x, L0_xattn_qln_w, L0_xattn_qln_b, L0_xattn_kln_w, L0_xattn_kln_b, L0_xattn_qxln_w, L0_xattn_qxln_b, L0_xattn_kxln_w, L0_xattn_kxln_b, L0_xattn_wproj, L0_xattn_proj_w_scale, L0_xattn_proj_in_scale, L0_xattn_proj_smooth)
    x = x + jnp.tanh(g_ffn[0]) * _L0_ffn_ref(_layernorm(x, axis=-1), L0_ffn_router_w, L0_ffn_gate_up_proj, L0_ffn_down_proj, L0_ffn_shared_gate_w, L0_ffn_shared_up_w, L0_ffn_shared_down_w)
    return x

_drawn_inputs = setup_inputs


def setup_inputs(seed=0):
    import zlib

    import numpy as np

    out = dict(_drawn_inputs(seed))
    spreads = {'L0_xattn_ln_w': (1.0, 0.6),
     'L0_xattn_ln_b': (0.0, 0.328),
     'L0_xattn_q_in_scale': (0.05000000074505806, 0.6),
     'L0_xattn_qx_in_scale': (0.05000000074505806, 0.6),
     'L0_xattn_k_in_scale': (0.05000000074505806, 0.6),
     'L0_xattn_v_in_scale': (0.05000000074505806, 0.6),
     'L0_xattn_qln_w': (1.0, 0.6),
     'L0_xattn_qln_b': (0.0, 0.8),
     'L0_xattn_kln_w': (1.0, 0.6),
     'L0_xattn_kln_b': (0.0, 2.0),
     'L0_xattn_qxln_w': (1.0, 0.6),
     'L0_xattn_qxln_b': (0.0, 0.8),
     'L0_xattn_kxln_w': (1.0, 0.6),
     'L0_xattn_kxln_b': (0.0, 2.0),
     'L0_xattn_proj_smooth': (0.05000000074505806, 0.6)}
    factors = {'L0_ffn_router_w': 7.05,
     'L0_ffn_gate_up_proj': 6.601,
     'L0_ffn_down_proj': 6.599,
     'L0_ffn_shared_gate_w': 8.0,
     'L0_ffn_shared_up_w': 8.0,
     'L0_ffn_shared_down_w': 8.0}
    for name, (base, spread) in spreads.items():
        noise = np.random.default_rng([zlib.crc32(name.encode()), seed]).standard_normal(out[name].shape)
        drawn = base * np.exp(spread * noise) if base else spread * noise
        out[name] = jnp.asarray(drawn.astype(out[name].dtype))
    for name, factor in factors.items():
        out[name] = (out[name] * factor).astype(out[name].dtype)
    return out
```

```python
from contextlib import ExitStack

import concourse.bass as bass
from concourse import mybir

ALU = mybir.AluOpType
ACT = mybir.ActivationFunctionType
AX_X = mybir.AxisListType.X
AX_XY = mybir.AxisListType.XY
F32 = mybir.dt.float32
F16 = mybir.dt.float16
BF16 = mybir.dt.bfloat16
U16 = mybir.dt.uint16
I32 = mybir.dt.int32

P = 128
B, S, H = 8, 256, 256
SC = 1601
G, HPG, D = 8, 2, 128
CK = H // P
ST = S // P
CT = (SC + P - 1) // P
LAST = SC - (CT - 1) * P
NT = ST + CT
Q = HPG * S
GW = 2 * HPG * D + 2 * D
VW = D + 1
SCALE = float(D) ** -0.5
EPS = 1e-5
FP8_MAX = 448.0
E, I = 8, 512
FC = I // P
LEAD = 2
RING = 3

STEP_JOBS = {0: ["SP0", "KV0"], 1: ["SP1", "KV1"], 2: ["KV2", "KV3"], 3: ["KV4", "KV5"], 4: ["KV6", "ST0"], 5: ["OT", "ST1"],
             6: ["MS0", "MS1"], 7: ["KT0"], 8: ["NS", "KT1"], 9: ["MX0", "MX1"], 10: ["MX2", "MX3"],
             11: ["MX4"], 12: ["MX5", "MX6"], 13: ["MX7"], 14: ["NC"]}
ROUND_JOBS = {13: ["XA0", "XA1"]}
OUTPUT_JOBS = {5: ["PJ0"], 6: ["PJ1"]}
PREP_JOBS = 25
ROW_JOBS = G * (PREP_JOBS + 1) + 4
KV_TILES = [(2 * j, 2) for j in range(CT // 2)] + [(CT - 1, 1)]
KT_TILES = [(0, 8), (8, 5)]
MX_STARTS = [0, 400, 800, SC - 401]
MX_W = 401


def rows_of(t):
    return LAST if t == CT - 1 else P


def body_jobs(attend, prep, ot, phase_a, pj):
    steps = []
    for k in range(NT):
        names = [n for n in STEP_JOBS.get(k, []) if (ot if n == "OT" else prep)]
        if phase_a:
            names += ROUND_JOBS.get(k, [])
        if pj:
            names += OUTPUT_JOBS.get(k, [])
        steps.append(names)
    return steps


class Jobs:

    def __init__(self, half, const):
        self.half, self.const = half, const

    def slot(self):
        return self.const % 2

    def released_before(self):
        return self.half + self.const // 2

    def ready(self):
        return self.half * 2 + (self.const + 1)

    def back(self, n):
        return Jobs(self.half, self.const - n)

    def step(self):
        self.const += 1


def plan(engine, fori):
    every = PREP_JOBS + 1
    engine.body(-1, G - 1, Jobs(0, 0), attend=False, phase_a=True, new_row=True, ot=False)
    at = PREP_JOBS + 2
    engine.body(0, 0, Jobs(0, at), ot=False)
    at += PREP_JOBS

    def rest(b, last):
        half = b * (ROW_JOBS // 2)
        engine.body(b, 1, Jobs(half, at))
        with fori(0, 2) as i:
            engine.body(b, i * 2 + 2, Jobs(half + i * every, at + every), parity=0, pair=i + 1)
            engine.body(b, i * 2 + 3, Jobs(half + i * every, at + 2 * every), parity=1, pair=i + 1)
        engine.body(b, 6, Jobs(half, at + 5 * every), phase_a=not last)
        engine.body(b, 7, Jobs(half, at + 6 * every + (0 if last else 2)), prep=not last, new_row=not last)
        return half, at + 7 * every + (0 if last else 2)

    with fori(0, B - 1) as b:
        half, n = rest(b, False)
        engine.body(b + 1, 0, Jobs(half, n), pj=True)
    half, n = rest(B - 1, True)
    engine.tail(B - 1, Jobs(half, n - PREP_JOBS))


NEWTON = 3
RSQRT_STEPS = 1 + 3 * NEWTON


def rsqrt(nc, out, v, t, wait):
    yield wait(nc.vector.tensor_scalar(out.bitcast(I32), v.bitcast(I32), -0.5, float(0x5F3759DF), ALU.mult, ALU.add))
    for _ in range(NEWTON):
        yield wait(nc.vector.tensor_tensor(t, out, out, ALU.mult))
        yield wait(nc.vector.scalar_tensor_tensor(out=t, in0=t, scalar=-0.5, in1=v, op0=ALU.mult, op1=ALU.mult))
        yield wait(nc.vector.scalar_tensor_tensor(out=out, in0=t, scalar=1.5, in1=out, op0=ALU.add, op1=ALU.mult))


MOMENT_STEPS = 4 + RSQRT_STEPS


def moments(nc, stats, n, mean, rstd, tmp, eps, wait):
    me, mo, ve, vo = (stats[:, :, i] for i in (1, 4, 2, 5))
    nc.vector.tensor_tensor(tmp[0], me, mo, ALU.add)
    nc.vector.tensor_tensor(tmp[1], me, mo, ALU.subtract)
    yield wait(nc.vector.tensor_tensor(tmp[2], ve, vo, ALU.add))
    nc.vector.tensor_scalar(mean, tmp[0], 0.5, None, ALU.mult)
    yield wait(nc.vector.scalar_tensor_tensor(out=tmp[3], in0=tmp[1], scalar=0.25, in1=tmp[1], op0=ALU.mult, op1=ALU.mult))
    yield wait(nc.vector.scalar_tensor_tensor(out=tmp[3], in0=tmp[2], scalar=1.0 / n, in1=tmp[3], op0=ALU.mult, op1=ALU.add))
    yield wait(nc.vector.tensor_tensor(tmp[3], tmp[3], eps, ALU.add))
    yield from rsqrt(nc, rstd, tmp[3], tmp[2], wait)


def attention_block(nc, a, x1_dram, inv_smooth):
    with ExitStack() as ctx:
        def sb(name, shape, dt):
            return ctx.enter_context(nc.sbuf_tensor(name, shape, dt))

        def sem(name):
            return ctx.enter_context(nc.semaphore(name))

        ident32 = sb("ident32", [P, P], F32)
        ident16 = sb("ident16", [P, P], F16)
        identb = sb("identb", [P, P], BF16)
        ones_row = sb("ones_row", [1, P], BF16)
        w_self = sb("w_self", [P, CK, G * GW], F16)
        wkv_hi = sb("wkv_hi", [P, CK, G * 2 * D], F16)
        wkv_lo = sb("wkv_lo", [P, CK, G * 2 * D], F16)
        w_proj = sb("w_proj", [P, 4 * G, H], F16)
        cols = sb("cols", [P, 32], F32)
        inv_scale = sb("inv_scale", [P, 4, H], F32)
        lnw_bc = sb("lnw_bc", [P, H], F32)
        lnb_bc = sb("lnb_bc", [P, H], F32)
        eps_w = sb("eps_w", [P, 10 + CT], F32)
        COL = {"in_scale": 0, "qw": 8, "qb": 9, "kw": 10, "kb": 11, "xw": 12, "xb": 13, "cw": 14, "cb": 15,
               "wq_s": 16, "wk_s": 17, "wx_s": 18, "wv_s": 19, "pw_s": 20, "pin_s": 21, "gate": 22, "coef": 23,
               "e0": 24}

        def col(name, i=0, rows=P):
            return cols[0:rows, COL[name] + i:COL[name] + i + 1]

        w_loaded = [sem(f"w{i}_loaded") for i in range(4)]
        small_loaded = sem("small_loaded")
        w_part = sem("w_part")
        w_center_step = sem("w_center_step")
        w_centered = sem("w_centered")
        smooth_in_loaded = sem("smooth_in_loaded")
        smooth_inverted = sem("smooth_inverted")
        inv_stored = sem("inv_stored")
        w_hi = sem("w_hi")
        w_lo = sem("w_lo")
        zeroed = sem("zeroed")
        ident_made = sem("ident_made")
        eps_step = sem("eps_step")
        coef_step = sem("coef_step")

        WC = 2048
        loads = []
        for c in range(CK):
            for n in range(G * GW // WC):
                loads.append((a["w_self"][c * P:(c + 1) * P, n * WC:(n + 1) * WC], w_self[:, c, n * WC:(n + 1) * WC], None))
            loads.append((a["w_kv"][c * P:(c + 1) * P, :], wkv_hi[:, c, :], wkv_lo[:, c, :]))
        for n in range(4):
            w = 4 * G // 4
            loads.append((a["w_proj"][:, n * w:(n + 1) * w, :].rearrange("p c n -> p (c n)"),
                          w_proj[:, n * w:(n + 1) * w, :].rearrange("p c n -> p (c n)"), None))
        with nc.sbuf_tensor("w_stage", [P, 4, WC], F32) as w_stage, \
                nc.sbuf_tensor("w_mean", [P, 2, G], F32) as w_mean, nc.sbuf_tensor("scale_in", [P, 4, H], F32) as scale_in, \
                nc.sbuf_tensor("smooth_in", [P, 2, G * 4 * D // P], F32) as smooth_in, nc.Block() as block:
            @block.sync
            def _(sp):
                spread = "g (q n) -> (g q) n"
                sp.dma_start(smooth_in[:, 0], a["smooth"].rearrange(spread, n=G * 4 * D // P)).then_inc(smooth_in_loaded, 16)
                sp.wait_ge(smooth_inverted, 1)
                sp.dma_start(inv_smooth.rearrange(spread, n=G * 4 * D // P), smooth_in[:, 1]).then_inc(inv_stored, 16)
                for src, dst in ((a["cols"], cols[:, 0:COL["coef"]]),
                                 (a["scales"].partition_broadcast(P), scale_in[:]),
                                 (a["ln_w"].partition_broadcast(P), lnw_bc[:]),
                                 (a["ln_b"].partition_broadcast(P), lnb_bc[:])):
                    sp.dma_start(dst, src).then_inc(small_loaded, 16)
                for n, (src, hi, lo) in enumerate(loads):
                    if n >= 4:
                        sp.wait_ge(w_part, n - 3)
                    sp.dma_start(w_stage[:, n % 4, :], src).then_inc(w_loaded[n % 4], 16)
                sp.wait_ge(inv_stored, 16)

            @block.scalar
            def _(act):
                seen = 0
                for n, (src, hi, lo) in enumerate(loads):
                    if lo is None:
                        continue
                    seen += 1
                    act.wait_ge(w_centered, seen)
                    nc.scalar.activation(hi, w_stage[:, n % 4, :], ACT.Copy).then_inc(w_hi, 1)
                act.wait_ge(small_loaded, 64)
                nc.scalar.activation(col("coef"), col("gate"), ACT.Tanh).then_inc(coef_step, 1)

            @block.vector
            def _(dve):
                dve.wait_ge(smooth_in_loaded, 16)
                nc.vector.reciprocal(smooth_in[:, 1], smooth_in[:, 0]).then_inc(smooth_inverted, 1)
                seen_hi = 0
                for n, (src, hi, lo) in enumerate(loads):
                    dve.wait_ge(w_loaded[n % 4], 16 * (n // 4 + 1))
                    if lo is None:
                        nc.vector.tensor_copy(hi, w_stage[:, n % 4, :]).then_inc(w_part, 1)
                    else:
                        seen_hi += 1
                        k_cols = w_stage[:, n % 4, :].rearrange("p (g s n) -> p g s n", s=2, n=D)[:, :, 0, :]
                        nc.vector.tensor_reduce(w_mean[:, 0, :], k_cols, AX_X, ALU.add).then_inc(w_center_step, 1)
                        dve.wait_ge(w_center_step, seen_hi * 2 - 1)
                        nc.vector.tensor_scalar(w_mean[:, 1, :], w_mean[:, 0, :], 1.0 / D, None, ALU.mult).then_inc(w_center_step, 1)
                        dve.wait_ge(w_center_step, seen_hi * 2)
                        nc.vector.tensor_tensor(k_cols, k_cols, w_mean[:, 1, :].unsqueeze(2).to_broadcast([P, G, D]), ALU.subtract)\
                            .then_inc(w_centered, 1)
                        dve.wait_ge(w_hi, seen_hi)
                        nc.vector.tensor_tensor(lo, w_stage[:, n % 4, :], hi, ALU.subtract).then_inc(w_part, 1)
                dve.wait_ge(small_loaded, 64)
                nc.vector.reciprocal(inv_scale[:], scale_in[:])
                nc.vector.tensor_tensor(cols[:, 24:27], cols[:, 16:19], cols[:, 16:19], ALU.mult).then_inc(eps_step, 1)
                dve.wait_ge(eps_step, 1)
                nc.vector.reciprocal(cols[:, 27:30], cols[:, 24:27]).then_inc(eps_step, 1)
                nc.vector.memset(eps_w[:], EPS).then_inc(eps_step, 1)
                dve.wait_ge(eps_step, 3)
                for i in range(10):
                    w = [0, 0, 1, 2, 2][i % 5]
                    last = nc.vector.tensor_scalar(eps_w[:, i:i + 1], cols[:, 27 + w:28 + w], EPS, None, ALU.mult)
                dve.wait_ge(coef_step, 1)
                nc.vector.scalar_tensor_tensor(out=cols[:, 30:31], in0=col("pw_s"), scalar=col("pin_s"), in1=col("coef"),
                                               op0=ALU.mult, op1=ALU.mult).then_inc(coef_step, 1)

            @block.gpsimd
            def _(pool):
                nc.gpsimd.memset(ident32[:], 0.0).then_inc(zeroed, 1)
                nc.gpsimd.memset(ones_row[:], 1.0).then_inc(zeroed, 1)
                pool.wait_ge(zeroed, 2)
                nc.gpsimd.affine_select(out=ident32[:], in_=ident32[:], compare_op=ALU.not_equal, fill=1.0, base=0,
                                        pattern=[[-1, P]], channel_multiplier=1).then_inc(ident_made, 1)
                pool.wait_ge(ident_made, 1)
                nc.gpsimd.tensor_copy(ident16[:], ident32[:]).then_inc(ident_made, 1)
                nc.gpsimd.tensor_copy(identb[:], ident32[:]).then_inc(ident_made, 1)
        COL["coef"] = 30

        catT = sb("catT", [P, 4 * G, S], F16)
        ctx_in = sb("ctx_in", [P, SC], F32)
        ctx_hi = sb("ctx_hi", [P, CK, SC], F16)
        ctx_lo = sb("ctx_lo", [P, CK, SC], F16)
        xq_hi = sb("xq_hi", [P, 4, CK, S], F16)
        xq_lo = sb("xq_lo", [P, 4, CK, S], F16)
        xt = sb("xt", [P, ST, H], F32)
        x_res = sb("x_res", [P, ST, H], F32)
        x_stats = sb("x_stats", [P, ST, 6], F32)
        x_mean = sb("x_mean", [P, ST], F32)
        eps_x = sb("eps_x", [P, ST], F32)
        x_rstd = sb("x_rstd", [P, ST], F32)
        x_tmp = sb("x_tmp", [P, 4, ST], F32)
        smooth = sb("smooth", [P, 2, 4 * D], F32)
        yo = sb("yo", [P, 1024], BF16)
        q_mag = sb("q_mag", [P, 1024], BF16)
        q_sum = sb("q_sum", [P, 1024], F32)
        rq = sb("rq", [P, ST, 1024], BF16)
        ro = sb("ro", [P, 1024], BF16)
        raw_self = sb("raw_self", [P, ST, GW], F32)
        raw_k = sb("raw_k", [P, CT, D], F32)
        stats = sb("stats", [P, 10 + CT, 6], F32)
        st_a = sb("st_a", [P, 10 + CT], F32)
        st_b = sb("st_b", [P, 10 + CT], F32)
        st_c = sb("st_c", [P, 10 + CT], F32)
        st_d = sb("st_d", [P, 10 + CT], F32)
        mean = sb("mean", [P, 10 + CT], F32)
        rstd = sb("rstd", [P, 10 + CT], F32)
        selfT_f = sb("selfT_f", [P, 5, S], F32)
        kxT_f = sb("kxT_f", [P, SC], F32)
        selfT_hi = sb("selfT_hi", [P, 2, 5, S], F16)
        selfT_lo = sb("selfT_lo", [P, 2, 5, S], F16)
        kxT_hi = sb("kxT_hi", [P, 2, SC], F16)
        kxT_lo = sb("kxT_lo", [P, 2, SC], F16)
        v_hi = sb("v_hi", [P, 2, NT, VW], F16)
        v_lo = sb("v_lo", [P, 2, NT, D], F16)
        neg_max = sb("neg_max", [1, 2, 2 * Q], BF16)
        mx = sb("mx", [P, 2, 8], F32)
        mx_neg = sb("mx_neg", [P, 8], BF16)
        p_f = sb("p_f", [P, RING, Q], F32)
        p_hi = sb("p_hi", [P, RING, Q], F16)
        p_lo = sb("p_lo", [P, RING, Q], F16)
        o_rinv = sb("o_rinv", [P, 2, 4], F32)
        score = ctx.enter_context(nc.psum_tensor("score", [P, 2, 512], F32))
        o_ps = ctx.enter_context(nc.psum_tensor("o_ps", [P, 2, 512], F32))
        work = ctx.enter_context(nc.psum_tensor("work", [P, 2, 1024], F32))

        work_ready = sem("work_ready")
        slot_free = [sem("slot0_free"), sem("slot1_free")]
        x_loaded = sem("x_loaded")
        ctx_loaded = sem("ctx_loaded")
        smooth_loaded = [sem("smooth0_loaded"), sem("smooth1_loaded")]
        xres_loaded = sem("xres_loaded")
        x1_stored = sem("x1_stored")
        x_step = sem("x_step")
        xq_hi_done = sem("xq_hi_done")
        ctx_hi_done = sem("ctx_hi_done")
        ctx_split = sem("ctx_split")
        raw_self_done = sem("raw_self_done")
        vself_hi_done = sem("vself_hi_done")
        kv_evac = sem("kv_evac")
        stat_step = sem("stat_step")
        self_norm = sem("self_norm")
        k_norm = sem("k_norm")
        selfT_hi_done = sem("selfT_hi_done")
        kxT_hi_done = sem("kxT_hi_done")
        selfT_lo_done = sem("selfT_lo_done")
        kxT_lo_done = sem("kxT_lo_done")
        mx_done = sem("mx_done")
        mx_step = sem("mx_step")
        scores_done = sem("scores_done")
        exp_done = sem("exp_done")
        plo_dve = sem("plo_dve")
        plo_pool = sem("plo_pool")
        p_free = sem("p_free")
        o_done = sem("o_done")
        o_recip = sem("o_recip")
        o_free = sem("o_free")
        q_step = sem("q_step")
        ro_done = sem("ro_done")
        init_done = sem("init_done")

        EXP_CREDIT = 2
        CTX_HI_STEPS, CTX_LO_STEPS = (8, 11), (9, 12)
        DVE_LO = 8
        POOL_LO = NT - DVE_LO

        def released(jobs):
            return slot_free[jobs.slot()], jobs.released_before() + 1

        def parity_of(g, parity):
            return g % 2 if parity is None else parity

        class Body:

            def index(self, b, g, parity, pair):
                self.b, self.g = b, g
                self.at = b * G + g if not isinstance(b, int) or b >= 0 else None
                self.pr = b * G + g + 1 if self.at is not None else 0
                self.ap = parity_of(g, parity)
                self.pp = 1 - self.ap
                self.pair = b * (G // 2) + (g // 2 if pair is None else pair)

        def order(steps, attend, phase_a):
            if attend or not phase_a:
                return steps
            return [ROUND_JOBS[13]] + [[n for n in names if n[:2] != "XA"] for names in steps]

        class PE(Body):
            def __init__(self, pe):
                self.pe, self.seen = pe, {}

            def start(self, jobs):
                if not (isinstance(jobs.half, int) and jobs.released_before() == 0):
                    self.pe.wait_ge(slot_free[jobs.slot()], jobs.released_before())
                return work[:, jobs.slot(), :]

            def job(self, name, jobs):
                pe, w = self.pe, self.start(jobs)
                j = int(name[2:]) if name[2:] else 0
                kind, pp = name[:2], self.pp
                if kind == "XA":
                    pe.wait_ge(x_step, (self.b + 1) * X_STEPS + X_STEPS)
                    wb = w[:, 0:512].bitcast(BF16).rearrange("p (n s) -> p n s", s=S)
                    for st in range(ST):
                        for n in range(4):
                            o = slice((j * 4 + n) * P, (j * 4 + n + 1) * P)
                            last = nc.tensor.transpose(wb[:, n, st * P:(st + 1) * P], rq[:, st, o], identb[:])
                elif kind == "SP":
                    if j == 0 and self.new_row:
                        pe.wait_ge(*self.seen["XA1"])
                    for lo_col, n, t in ((0, 2 * D, 0), (2 * D, D, 1), (3 * D, D, 2), (4 * D, 2 * D, 3)):
                        for i in range(2 * CK):
                            src = (xq_hi, xq_lo)[i % 2]
                            last = nc.tensor.matmul(w[:, lo_col:lo_col + n], src[:, t, i // 2, j * P:(j + 1) * P],
                                                    w_self[:, i // 2, bass.ds(self.wg * GW + lo_col, n)],
                                                    start=(i == 0), stop=(i == 2 * CK - 1))
                elif kind == "KV":
                    pe.wait_ge(ctx_split, (self.row + 1) * CK)
                    t0, n = KV_TILES[j]
                    for t in range(t0, t0 + n):
                        r = rows_of(t)
                        o = w[0:r, (t - t0) * 2 * D:(t - t0 + 1) * 2 * D]
                        for i in range(3 * CK):
                            c, part = i // 3, i % 3
                            last = nc.tensor.matmul(o, (ctx_hi, ctx_hi, ctx_lo)[part][:, c, t * P:t * P + r],
                                                    (wkv_hi, wkv_lo, wkv_hi)[part][:, c, bass.ds(self.wg * 2 * D, 2 * D)],
                                                    start=(i == 0), stop=(i == 3 * CK - 1))
                elif kind == "ST":
                    pe.wait_ge(self_norm, self.pr * ST + j + 1)
                    for i, c in enumerate((0, 1, 2, 4, 5)):
                        last = nc.tensor.transpose(w[:, i * P:(i + 1) * P], raw_self[:, j, c * P:(c + 1) * P], ident32[:])
                elif kind == "KT":
                    t0, n = KT_TILES[j]
                    pe.wait_ge(k_norm, self.pr * 2 + (j + 1))
                    for t in range(t0, t0 + n):
                        r = rows_of(t)
                        last = nc.tensor.transpose(w[:, (t - t0) * P:(t - t0) * P + r], raw_k[0:r, t, :], ident32[0:r, 0:r])
                elif kind == "MX":
                    if j == 0:
                        pe.wait_ge(kxT_hi_done, self.pr * 2 + 2)
                    q = selfT_hi[:, pp, 3 + j // 4, ((j // 2) % 2) * P:((j // 2) % 2 + 1) * P]
                    for i in range(2):
                        c0 = MX_STARTS[(j % 2) * 2 + i]
                        last = nc.tensor.matmul(w[:, i * 512:i * 512 + MX_W], q, kxT_hi[:, pp, c0:c0 + MX_W], start=True, stop=True)
                elif kind == "MS":
                    if j == 0:
                        pe.wait_ge(selfT_hi_done, self.pr * ST + 2)
                    for st in range(ST):
                        last = nc.tensor.matmul(w[:, st * S:(st + 1) * S], selfT_hi[:, pp, j, st * P:(st + 1) * P],
                                                selfT_hi[:, pp, 2, :], start=True, stop=True)
                elif kind in ("NS", "NC"):
                    context = int(kind == "NC")
                    pe.wait_ge(mx_step, self.pr * 2 + (1 + context))
                    for i in range(4):
                        last = nc.tensor.matmul(w[0:1, i * P:(i + 1) * P], mx_neg[:, context * 4 + i:context * 4 + i + 1],
                                                identb[:], start=True, stop=True)
                elif kind == "OT":
                    pe.wait_ge(ro_done, self.ot)
                    wb = w.bitcast(BF16)
                    for i in range(8):
                        last = nc.tensor.transpose(wb[:, i * P:(i + 1) * P], ro[:, i * P:(i + 1) * P], identb[:])
                elif kind == "PJ":
                    if j == 0:
                        pe.wait_ge(*self.seen["OT0"])
                    for c in range(4 * G):
                        last = nc.tensor.matmul(w[:, 0:H], catT[:, c, j * P:(j + 1) * P], w_proj[:, c, :],
                                                start=(c == 0), stop=(c == 4 * G - 1))
                last.then_inc(work_ready, 1)
                self.seen[name if name[2:] else name + "0"] = released(jobs)
                jobs.step()

            def scores(self, k, ahead=0):
                pe, ap = self.pe, (self.pp if ahead else self.ap)
                a_ = self.pr if ahead else self.at
                t = k - ST
                r = P if k < ST else rows_of(t)
                tile = a_ * NT + k
                if k == 0:
                    pe.wait_ge(*self.seen["NS0"])
                    pe.wait_ge(selfT_lo_done, a_ * ST + 3)
                if k == ST:
                    pe.wait_ge(*released(self.nc_job))
                    pe.wait_ge(kxT_lo_done, a_ * 2 + 3)
                pe.wait_ge(exp_done, tile + 1)
                q = slice(0, 2) if k < ST else slice(3, 5)
                q_hi = selfT_hi[:, ap, q, :].rearrange("p h s -> p (h s)")
                q_lo = selfT_lo[:, ap, q, :].rearrange("p h s -> p (h s)")
                if k < ST:
                    k_hi, k_lo = (x[:, ap, 2, k * P:(k + 1) * P] for x in (selfT_hi, selfT_lo))
                else:
                    k_hi, k_lo = (x[:, ap, t * P:t * P + r] for x in (kxT_hi, kxT_lo))
                o = score[0:r, (ap + k) % 2, :]
                nc.tensor.matmul(o, k_hi, q_hi, start=True, stop=False)
                nc.tensor.matmul(o, k_hi, q_lo, start=False, stop=False)
                nc.tensor.matmul(o, k_lo, q_hi, start=False, stop=False)
                at = 0 if k < ST else Q
                nc.tensor.matmul(o, ones_row[:, 0:r], neg_max[:, ap, at:at + Q], start=False, stop=True).then_inc(scores_done, 1)

            def pv(self, k):
                pe, ap, a_ = self.pe, self.ap, self.at
                t = k - ST
                r = P if k < ST else rows_of(t)
                if k == 0:
                    pe.wait_ge(o_free, a_ * 2 + 1)
                if k == ST:
                    pe.wait_ge(o_free, a_ * 2 + 2)
                if k % 2 == 0:
                    pe.wait_ge(plo_dve, a_ * DVE_LO + (k // 2 + 1))
                else:
                    pe.wait_ge(plo_pool, a_ * POOL_LO + (k // 2 + 1))
                first, final = k in (0, ST), k in (ST - 1, NT - 1)
                for j in range(4):
                    o = o_ps[:, j // 3, (j % 3) * VW:(j % 3) * VW + VW]
                    ph = p_hi[0:r, k % RING, j * P:(j + 1) * P]
                    pl = p_lo[0:r, k % RING, j * P:(j + 1) * P]
                    nc.tensor.matmul(o, ph, v_hi[0:r, ap, k, :], start=first and j in (0, 3), stop=False, skip_group_check=True)
                    nc.tensor.matmul(o[:, 0:D], ph, v_lo[0:r, ap, k, :], start=False, stop=False, skip_group_check=True)
                    last = nc.tensor.matmul(o, pl, v_hi[0:r, ap, k, :], start=False, stop=final, skip_group_check=True)
                last.then_inc(p_free, 1)

            def body(self, b, g, jobs, attend=True, prep=True, ot=True, phase_a=False, new_row=False, pj=False, parity=None, pair=None):
                self.index(b, g, parity, pair)
                self.row = b + 1 if new_row else b
                self.new_row = new_row
                self.wg = 0 if new_row else g + 1
                self.ot = self.at
                self.nc_job = jobs.back(1)
                steps = order(body_jobs(attend, prep, ot, phase_a, pj), attend, phase_a)
                for k, names in enumerate(steps):
                    if attend and k + LEAD < NT:
                        self.scores(k + LEAD)
                    if prep and k + LEAD >= NT and len(steps) == NT:
                        self.scores(k + LEAD - NT, 1)
                    for name in names:
                        self.job(name, jobs)
                    if attend:
                        self.pv(k)
                if not attend:
                    for k in range(LEAD):
                        self.scores(k, 1)

            def tail(self, b, jobs):
                self.ot = b * G + G
                for name in ("OT", "PJ0", "PJ1"):
                    self.job(name, jobs)

        class ACTE(Body):
            def __init__(self, act):
                self.act = act

            def job(self, name, jobs):
                act, w, pp = self.act, work[:, jobs.slot(), :], self.pp
                j = int(name[2:]) if name[2:] else 0
                kind = name[:2]
                free = slot_free[jobs.slot()]
                if kind not in ("MX", "MS", "PJ"):
                    act.wait_ge(work_ready, jobs.ready())
                if kind == "XA":
                    wb = w[:, 0:512].bitcast(BF16).rearrange("p (n s) -> p n s", s=S)
                    for i in range(4):
                        n = j * 4 + i
                        last = nc.scalar.activation(xq_hi[:, n // CK, n % CK, :], wb[:, i, :], ACT.Copy, scale=col("in_scale", n))
                    last.then_inc(xq_hi_done, 1)
                elif kind == "SP":
                    nc.scalar.activation(raw_self[:, j, :], w[:, 0:GW], ACT.Copy).then_inc(raw_self_done, 1)
                    nc.scalar.activation(v_hi[:, pp, j, 0:D], w[:, 3 * D:4 * D], ACT.Copy, scale=col("wv_s"))\
                        .then_inc(vself_hi_done, 1)
                elif kind == "KV":
                    t0, n = KV_TILES[j]
                    r = rows_of(t0)
                    o = w[0:r, 0:n * 2 * D].rearrange("p (t n) -> p t n", n=2 * D)
                    nc.scalar.activation(raw_k[0:r, t0:t0 + n, :], o[:, :, 0:D], ACT.Copy)
                    nc.scalar.activation(v_hi[0:r, pp, ST + t0:ST + t0 + n, 0:D], o[:, :, D:2 * D], ACT.Copy).then_inc(kv_evac, 1)
                elif kind == "ST":
                    if j == 0:
                        act.wait_ge(selfT_lo_done, self.pr * ST + 1)
                    for o, n, wb in ((0, 2, "q"), (2, 1, "k"), (3, 2, "x")):
                        last = nc.scalar.activation(selfT_f[:, o:o + n, j * P:(j + 1) * P],
                                                    w[:, o * P:(o + n) * P].rearrange("p (h s) -> p h s", s=P),
                                                    ACT.Identity, bias=col(wb + "b"), scale=col(wb + "w"))
                    last.then_inc(free, 1)
                elif kind == "KT":
                    if j == 0:
                        act.wait_ge(kxT_lo_done, self.pr * 2 + 1)
                    c0 = KT_TILES[j][0] * P
                    n = min(SC - c0, KT_TILES[j][1] * P)
                    nc.scalar.activation(kxT_f[:, c0:c0 + n], w[:, 0:n], ACT.Identity, bias=col("cb"), scale=col("cw"))\
                        .then_inc(free, 1)
                elif kind in ("NS", "NC"):
                    at = Q if kind == "NC" else 0
                    nc.scalar.activation(neg_max[:, pp, at:at + Q], w[0:1, 0:Q], ACT.Copy).then_inc(free, 1)
                elif kind == "OT":
                    self.out_turned(w, free)
                jobs.step()

            def split_ctx(self, c):
                self.act.wait_ge(ctx_loaded, self.b * (16 * CK) + 16 * (CK + c + 1))
                nc.scalar.activation(ctx_hi[:, c, :], ctx_in[:], ACT.Copy).then_inc(ctx_hi_done, 1)

            def out_turned(self, w, free):
                g = self.cat_g
                nc.scalar.activation(catT[:, bass.ds(g * 4, 4), :].rearrange("p c s -> p (c s)"), w.bitcast(BF16)[:, 0:1024],
                                     ACT.Copy).then_inc(free, 1)

            def exp(self, k, ahead=0):
                act, a_ = self.act, (self.pr if ahead else self.at)
                ap = self.pp if ahead else self.ap
                r = P if k < ST else rows_of(k - ST)
                tile = a_ * NT + k
                act.wait_ge(scores_done, tile + 1)
                act.wait_ge(p_free, tile + 1)
                s = score[0:r, (ap + k) % 2, :]
                nc.scalar.activation(p_f[0:r, k % RING, :], s, ACT.Exp, scale=SCALE)
                nc.scalar.activation(p_hi[0:r, k % RING, :], s, ACT.Exp, scale=SCALE).then_inc(exp_done, 1)

            def body(self, b, g, jobs, attend=True, prep=True, ot=True, phase_a=False, new_row=False, pj=False, parity=None, pair=None):
                self.index(b, g, parity, pair)
                self.cat_g = G - 1 if pj else g - 1
                steps = order(body_jobs(attend, prep, ot, phase_a, pj), attend, phase_a)
                if not attend:
                    for c in range(CK):
                        self.split_ctx(c)
                for k, names in enumerate(steps):
                    if attend and k + 1 < NT:
                        self.exp(k + 1)
                    if attend and prep and k + 1 == NT:
                        self.exp(0, 1)
                    for name in names:
                        self.job(name, jobs)
                    if attend and phase_a and k in CTX_HI_STEPS:
                        self.split_ctx(CTX_HI_STEPS.index(k))
                if not attend:
                    self.exp(0, 1)

            def tail(self, b, jobs):
                self.cat_g = G - 1
                self.job("OT", jobs)
                jobs.step()
                jobs.step()

        X_STEPS = 2 * (2 + MOMENT_STEPS) + 2 + 2 * (1 + 5)
        Q_STEPS = 4
        STAT_STEPS = 2 * (1 + MOMENT_STEPS)
        class DVE(Body):
            def __init__(self, dve):
                self.dve = dve

            def round_fp8(self, dst, y, wait, end):
                wait(nc.vector.tensor_scalar(y, y, FP8_MAX, -FP8_MAX, ALU.min, ALU.max))
                wait(nc.vector.tensor_scalar(q_mag[:].bitcast(U16), y.bitcast(U16), 0x7F80, 0x0040,
                                             ALU.bitwise_and, ALU.bitwise_or))
                wait(nc.vector.tensor_scalar(q_mag[:], q_mag[:], 1.5 * 2.0 ** -6, 2.0 ** 20, ALU.max, ALU.mult))
                yield
                wait(nc.vector.tensor_tensor(q_sum[:], y, q_mag[:], ALU.add))
                yield
                end(nc.vector.tensor_tensor(dst, q_sum[:], q_mag[:], ALU.subtract))

            def phase_a(self):
                dve, base = self.dve, (self.b + 1) * X_STEPS
                dve.wait_ge(x_loaded, (self.b + 1) * 16 + 16)
                n = [0]

                def wait(ins):
                    n[0] += 1
                    ins.then_inc(x_step, 1)
                    dve.wait_ge(x_step, base + n[0])

                for rnd in range(2):
                    for st in range(ST):
                        last = nc.vector.bn_stats(x_stats[:, st, :], xt[:, st, :])
                    wait(last)
                    for _ in moments(nc, x_stats[:], H, x_mean[:], x_rstd[:], [x_tmp[:, i] for i in range(4)], eps_x[:], wait):
                        pass
                    for st in range(ST):
                        last = nc.vector.tensor_scalar(xt[:, st, :], xt[:, st, :], x_mean[:, st:st + 1], x_rstd[:, st:st + 1],
                                                       ALU.subtract, ALU.mult)
                    wait(last)
                    yield
                wait(nc.vector.tensor_tensor(xt[:], xt[:], lnw_bc[:].unsqueeze(1).to_broadcast([P, ST, H]), ALU.mult))
                wait(nc.vector.tensor_tensor(xt[:], xt[:], lnb_bc[:].unsqueeze(1).to_broadcast([P, ST, H]), ALU.add))
                yield
                for st in range(ST):
                    wait(nc.vector.tensor_tensor(rq[:, st, :].rearrange("p (t n) -> p t n", t=4),
                                                 xt[:, st, :].unsqueeze(1).to_broadcast([P, 4, H]), inv_scale[:], ALU.mult))
                    yield
                    yield from self.round_fp8(rq[:, st, :], rq[:, st, :], wait, wait)
                    yield
                assert n[0] == X_STEPS

            def job(self, name, jobs):
                dve, w, pp = self.dve, work[:, jobs.slot(), :], self.pp
                j = int(name[2:]) if name[2:] else 0
                kind = name[:2]
                free = slot_free[jobs.slot()]
                if kind == "XA":
                    wb = w[:, 0:512].bitcast(BF16).rearrange("p (n s) -> p n s", s=S)
                    dve.wait_ge(xq_hi_done, (self.b + 1) * 2 + (j + 1))
                    for i in range(4):
                        n = j * 4 + i
                        last = nc.vector.scalar_tensor_tensor(
                            out=xq_lo[:, n // CK, n % CK, :], in0=wb[:, i, :], scalar=col("in_scale", n),
                            in1=xq_hi[:, n // CK, n % CK, :], op0=ALU.mult, op1=ALU.subtract)
                    last.then_inc(free, 1)
                elif kind == "SP":
                    dve.wait_ge(vself_hi_done, self.pr * ST + j + 1)
                    nc.vector.scalar_tensor_tensor(out=v_lo[:, pp, j, :], in0=w[:, 3 * D:4 * D], scalar=col("wv_s"),
                                                   in1=v_hi[:, pp, j, 0:D], op0=ALU.mult, op1=ALU.subtract).then_inc(free, 1)
                    for i, c in enumerate((0, 1, 2, 4, 5)):
                        last = nc.vector.bn_stats(stats[:, j * 5 + i, :], raw_self[:, j, c * P:(c + 1) * P])
                    if j == 1:
                        self.self_chain = self.norm_self(last)
                        next(self.self_chain)
                elif kind == "KV":
                    t0, n = KV_TILES[j]
                    r = rows_of(t0)
                    dve.wait_ge(kv_evac, self.pr * len(KV_TILES) + (j + 1))
                    o = w[0:r, 0:n * 2 * D].rearrange("p (t n) -> p t n", n=2 * D)
                    nc.vector.tensor_tensor(v_lo[0:r, pp, ST + t0:ST + t0 + n, :], o[:, :, D:2 * D],
                                            v_hi[0:r, pp, ST + t0:ST + t0 + n, 0:D], ALU.subtract).then_inc(free, 1)
                    for t in range(t0, t0 + n):
                        last = nc.vector.bn_stats(stats[0:r, 10 + t, :], raw_k[0:r, t, :])
                    if j == len(KV_TILES) - 1:
                        for _ in self.norms(last, 10, 10 + CT):
                            pass
                    elif j >= 2:
                        for _ in range(5):
                            next(self.self_chain, None)
                elif kind == "ST":
                    dve.wait_ge(*released(jobs))
                    tokens = slice(j * P, (j + 1) * P)
                    nc.vector.tensor_copy(selfT_hi[:, pp, :, tokens], selfT_f[:, :, tokens]).then_inc(selfT_hi_done, 1)
                    dve.wait_ge(selfT_hi_done, self.pr * ST + j + 1)
                    nc.vector.tensor_tensor(selfT_lo[:, pp, :, tokens], selfT_f[:, :, tokens], selfT_hi[:, pp, :, tokens],
                                            ALU.subtract).then_inc(selfT_lo_done, 1)
                elif kind == "KT":
                    dve.wait_ge(*released(jobs))
                    c0 = KT_TILES[j][0] * P
                    n = min(SC - c0, KT_TILES[j][1] * P)
                    nc.vector.tensor_copy(kxT_hi[:, pp, c0:c0 + n], kxT_f[:, c0:c0 + n]).then_inc(kxT_hi_done, 1)
                    if j == 1:
                        dve.wait_ge(kxT_hi_done, self.pr * 2 + 2)
                        nc.vector.tensor_tensor(kxT_lo[:, pp, c0:c0 + n], kxT_f[:, c0:c0 + n], kxT_hi[:, pp, c0:c0 + n],
                                                ALU.subtract).then_inc(kxT_lo_done, 1)
                elif kind == "MX":
                    dve.wait_ge(work_ready, jobs.ready())
                    spans = w.rearrange("p (i n) -> p i n", n=512)[:, :, 0:MX_W]
                    nc.vector.tensor_reduce(mx[:, j % 2, 4 + j // 2:5 + j // 2], spans, AX_XY, ALU.max).then_inc(free, 1)
                    if j == 7:
                        self.maxima(jobs)
                elif kind == "MS":
                    dve.wait_ge(work_ready, jobs.ready())
                    nc.vector.tensor_reduce(mx[:, 0, 2 * j:2 * j + ST], w[:, 0:ST * S].rearrange("p (t n) -> p t n", n=S),
                                            AX_X, ALU.max).then_inc(free, 1)
                    if j == 1:
                        dve.wait_ge(*released(jobs))
                        nc.vector.tensor_scalar(mx_neg[:, 0:4], mx[:, 0, 0:4], -1.0, None, ALU.mult).then_inc(mx_step, 1)
                elif kind == "PJ":
                    dve.wait_ge(work_ready, jobs.ready())
                    if j == 0:
                        dve.wait_ge(xres_loaded, self.pj * 16 + 16)
                    nc.vector.scalar_tensor_tensor(out=x_res[:, j, :], in0=w[:, 0:H], scalar=col("coef"), in1=x_res[:, j, :],
                                                   op0=ALU.mult, op1=ALU.add).then_inc(free, 1)
                jobs.step()

            def norms(self, last, lo, hi):
                dve, base = self.dve, self.pr * STAT_STEPS + (STAT_STEPS // 2 if lo else 0)
                n = [0]

                def wait(ins):
                    n[0] += 1
                    ins.then_inc(stat_step, 1)
                    dve.wait_ge(stat_step, base + n[0])
                wait(last)
                yield
                yield from moments(nc, stats[:, lo:hi], D, mean[:, lo:hi], rstd[:, lo:hi],
                                   [x[:, lo:hi] for x in (st_a, st_b, st_c, st_d)], eps_w[:, lo:hi], wait)
                assert n[0] * 2 == STAT_STEPS

            def norm_self(self, last):
                yield from self.norms(last, 0, 10)
                for st in range(ST):
                    for i, c in enumerate((0, 1, 2, 4, 5)):
                        n = st * 5 + i
                        o = raw_self[:, st, c * P:(c + 1) * P]
                        ins = nc.vector.tensor_scalar(o, o, mean[:, n:n + 1], rstd[:, n:n + 1], ALU.subtract, ALU.mult)
                    ins.then_inc(self_norm, 1)
                    yield

            def maxima(self, jobs):
                dve = self.dve
                dve.wait_ge(*released(jobs))
                nc.vector.tensor_tensor(mx[:, 0, 4:8], mx[:, 0, 4:8], mx[:, 1, 4:8], ALU.max).then_inc(mx_done, 1)
                dve.wait_ge(mx_done, self.pr + 1)
                nc.vector.tensor_scalar(mx_neg[:, 4:8], mx[:, 0, 4:8], -1.0, None, ALU.mult).then_inc(mx_step, 1)

            def low(self, k, ahead=0):
                r = P if k < ST else rows_of(k - ST)
                self.dve.wait_ge(exp_done, (self.pr if ahead else self.at) * NT + (k + 1 + EXP_CREDIT))
                nc.vector.tensor_tensor(p_lo[0:r, k % RING, :], p_f[0:r, k % RING, :], p_hi[0:r, k % RING, :], ALU.subtract)\
                    .then_inc(plo_dve, 1)

            def take_outputs(self, src, g):
                dve, a_ = self.dve, self.at
                dve.wait_ge(p_free, a_ * NT + (RING + (ST if src == 0 else NT)))
                if src == 0:
                    dve.wait_ge(smooth_loaded[self.ap], self.pair * 16 + 16)
                nc.vector.reciprocal(o_rinv[:, src, 0:3], o_ps[:, 0, D:3 * VW:VW])
                nc.vector.reciprocal(o_rinv[:, src, 3:4], o_ps[:, 1, D:D + 1]).then_inc(o_recip, 1)
                dve.wait_ge(o_recip, a_ * 2 + (src + 1))
                for j in range(4):
                    last = nc.vector.scalar_tensor_tensor(
                        out=yo[:, (src * 4 + j) * P:(src * 4 + j + 1) * P], in0=o_ps[:, j // 3, (j % 3) * VW:(j % 3) * VW + D],
                        scalar=o_rinv[:, src, j:j + 1], in1=smooth[:, self.ap, (src * 2 + j // 2) * D:(src * 2 + j // 2 + 1) * D],
                        op0=ALU.mult, op1=ALU.mult)
                last.then_inc(o_free, 1)

            def round_outputs(self, a_):
                dve, base, n = self.dve, a_ * Q_STEPS, [0]
                dve.wait_ge(o_free, a_ * 2 + 3)

                def wait(ins):
                    n[0] += 1
                    ins.then_inc(q_step, 1)
                    dve.wait_ge(q_step, base + n[0])
                yield from self.round_fp8(ro[:], yo[:], wait, lambda ins: ins.then_inc(ro_done, 1))
                assert n[0] == Q_STEPS

            def split_ctx(self, c):
                self.dve.wait_ge(ctx_hi_done, self.b * CK + (CK + c + 1))
                nc.vector.tensor_tensor(ctx_lo[:, c, :], ctx_in[:], ctx_hi[:, c, :], ALU.subtract).then_inc(ctx_split, 1)

            def body(self, b, g, jobs, attend=True, prep=True, ot=True, phase_a=False, new_row=False, pj=False, parity=None, pair=None):
                self.index(b, g, parity, pair)
                self.pj = b - 1
                tokens = self.phase_a() if phase_a else iter(())
                outputs = self.round_outputs(b * G + g - 1 if isinstance(g, int) and not pj else b * G + (g - 1)) if ot and not pj else iter(())
                if pj:
                    outputs = self.round_outputs((b - 1) * G + (G - 1))
                steps = order(body_jobs(attend, prep, ot, phase_a, pj), attend, phase_a)
                if not attend:
                    for _ in tokens:
                        pass
                    for c in range(CK):
                        self.split_ctx(c)
                for k, names in enumerate(steps):
                    if attend:
                        if k % 2 == 1:
                            self.low(k + 1)
                        if prep and k + 1 == NT:
                            self.low(0, 1)
                        if k == ST:
                            self.take_outputs(0, g)
                    for name in names:
                        self.job(name, jobs)
                    if attend:
                        if k != ST:
                            next(outputs, None)
                        next(tokens, None)
                    if attend and phase_a and k in CTX_LO_STEPS:
                        self.split_ctx(CTX_LO_STEPS.index(k))
                if attend:
                    assert next(outputs, None) is None and next(tokens, None) is None
                    self.take_outputs(1, g)
                else:
                    self.low(0, 1)

            def tail(self, b, jobs):
                self.pj = b
                for _ in self.round_outputs(b * G + (G - 1)):
                    pass
                jobs.step()
                self.job("PJ0", jobs)
                self.job("PJ1", jobs)

        NORM_TILES = {5: (0, 8), 6: (8, CT)}

        class Pool(Body):
            def __init__(self, pool):
                self.pool = pool

            def body(self, b, g, jobs, attend=True, prep=True, ot=True, phase_a=False, new_row=False, pj=False, parity=None, pair=None):
                pool = self.pool
                self.index(b, g, parity, pair)
                steps = order(body_jobs(attend, prep, ot, phase_a, pj), attend, phase_a)
                for k, names in enumerate(steps):
                    if attend and k % 2 == 0 and k + 1 < NT:
                        m = k + 1
                        r = P if m < ST else rows_of(m - ST)
                        pool.wait_ge(exp_done, self.at * NT + (m + 1 + EXP_CREDIT))
                        nc.gpsimd.tensor_tensor(p_lo[0:r, m % RING, :], p_f[0:r, m % RING, :], p_hi[0:r, m % RING, :],
                                                ALU.subtract).then_inc(plo_pool, 1)
                    if prep and k == 5:
                        pool.wait_ge(stat_step, (self.pr + 1) * STAT_STEPS)
                    if prep and k in NORM_TILES:
                        t0, t1 = NORM_TILES[k]
                        r = P
                        o = raw_k[0:r, t0:t1, :]
                        nc.gpsimd.tensor_tensor(o, o, rstd[0:r, 10 + t0:10 + t1].unsqueeze(2).to_broadcast([r, t1 - t0, D]),
                                                ALU.mult).then_inc(k_norm, 1)
                    for name in names:
                        if name == "KT0":
                            j = 0
                            c0 = KT_TILES[j][0] * P
                            n = min(SC - c0, KT_TILES[j][1] * P)
                            pool.wait_ge(kxT_hi_done, self.pr * 2 + (j + 1))
                            nc.gpsimd.tensor_tensor(kxT_lo[:, self.pp, c0:c0 + n], kxT_f[:, c0:c0 + n],
                                                    kxT_hi[:, self.pp, c0:c0 + n], ALU.subtract).then_inc(kxT_lo_done, 1)
                        jobs.step()

            def tail(self, b, jobs):
                pass

        class SP(Body):
            def __init__(self, sp):
                self.sp = sp

            def load_chunk(self, row, c):
                self.sp.dma_start(ctx_in[:], a["ctxT"][bass.ds(row, 1), c * P:(c + 1) * P, :].rearrange("a p n -> p (a n)"))\
                    .then_inc(ctx_loaded, 16)

            def load_tokens(self, row, to, done):
                self.sp.dma_start(to[:], a["x"][bass.ds(row, 1)].rearrange("a (t p) n -> p (a t) n", p=P)).then_inc(done, 16)

            def body(self, b, g, jobs, attend=True, prep=True, ot=True, phase_a=False, new_row=False, pj=False, parity=None, pair=None):
                sp = self.sp
                self.index(b, g, parity, pair)
                if not attend:
                    sp.wait_ge(init_done, 2)
                    self.load_tokens(0, xt, x_loaded)
                    self.load_chunk(0, 0)
                    sp.wait_ge(ctx_split, 1)
                    self.load_chunk(0, 1)
                if isinstance(g, int) and g == 1 and not (isinstance(b, int) and b == B - 1):
                    sp.wait_ge(x_step, (b + 1) * X_STEPS)
                    self.load_tokens(b + 1, xt, x_loaded)
                    sp.wait_ge(ctx_split, (b + 1) * CK)
                    self.load_chunk(b + 1, 0)
                if phase_a and attend:
                    sp.wait_ge(ctx_split, (b + 1) * CK + 1)
                    self.load_chunk(b + 1, 1)
                if prep:
                    gp = 0 if new_row else g + 1
                    if attend:
                        sp.wait_ge(o_free, self.at * 2 + 1)
                    sp.dma_start(smooth[:, self.pp, :], inv_smooth[bass.ds(gp, 1), :].partition_broadcast(P).rearrange("p a n -> p (a n)"))\
                        .then_inc(smooth_loaded[self.pp], 16)
                if pj:
                    names = sum(body_jobs(attend, prep, ot, phase_a, pj), [])
                    self.residual(b - 1, Jobs(jobs.half, jobs.const + names.index("PJ1")))

            def residual(self, row, pj1):
                sp = self.sp
                sp.wait_ge(x1_stored, row * 16 + 16)
                self.load_tokens(row, x_res, xres_loaded)
                sp.wait_ge(*released(pj1))
                sp.dma_start(x1_dram[bass.ds(row, 1)].rearrange("a (t p) n -> p (a t) n", p=P), x_res[:]).then_inc(x1_stored, 16)

            def tail(self, b, jobs):
                self.residual(b, Jobs(jobs.half, jobs.const + 2))

        with nc.Block() as block:
            @block.sync
            def _(sp):
                plan(SP(sp), sp.Fori)
                sp.wait_ge(x1_stored, 16 * B + 16)

            @block.tensor
            def _(pe):
                pe.wait_ge(init_done, 2)
                plan(PE(pe), pe.Fori)

            @block.scalar
            def _(act):
                act.wait_ge(init_done, 2)
                plan(ACTE(act), act.Fori)

            @block.vector
            def _(dve):
                nc.vector.memset(v_hi[:], 1.0).then_inc(exp_done, EXP_CREDIT)
                nc.vector.memset(v_lo[:], 0.0).then_inc(p_free, RING)
                nc.vector.memset(stats[:], 0.0).then_inc(init_done, 1)
                nc.vector.memset(eps_x[:], EPS).then_inc(o_free, 1)
                nc.vector.memset(x_mean[:], 0.0).then_inc(x1_stored, 16)
                nc.vector.memset(q_sum[:, 0:1], 0.0).then_inc(selfT_lo_done, 1)
                nc.vector.memset(q_mag[:, 0:1], 0.0).then_inc(kxT_lo_done, 1)
                nc.vector.memset(raw_k[:], 0.0).then_inc(init_done, 1)
                dve.wait_ge(init_done, 2)
                plan(DVE(dve), dve.Fori)

            @block.gpsimd
            def _(pool):
                plan(Pool(pool), pool.Fori)


TG = 4
NG = B * ST // TG
TOK = TG * P
U = E + 1
CHUNKS = U * FC


def experts_block(nc, a, x1, out):
    with ExitStack() as ctx:
        def sb(name, shape, dt):
            return ctx.enter_context(nc.sbuf_tensor(name, shape, dt))

        def sem(name):
            return ctx.enter_context(nc.semaphore(name))

        ident = sb("e_ident", [P, P], F32)
        gu_hi = sb("gu_hi", [P, CK, U * 2 * I], F16)
        gu_lo = sb("gu_lo", [P, CK, U * 2 * I], F16)
        dn_hi = sb("dn_hi", [P, FC, U * H], F16)
        dn_lo = sb("dn_lo", [P, FC, U * H], F16)
        router = sb("router", [P, CK, E], F32)
        gate = sb("gate", [P, 2], F32)
        order = sb("order", [P, TG, E], F32)
        w_loaded = [sem(f"ew{i}_loaded") for i in range(4)]
        w_hi = sem("ew_hi")
        w_lo = sem("ew_lo")
        small_loaded = sem("e_small_loaded")
        ident_step = sem("e_ident_step")

        WC = 1024
        loads = []
        for u in range(U):
            for c in range(CK):
                w = slice(u * 2 * I, (u + 1) * 2 * I)
                loads.append((a["w_gu"][u, c * P:(c + 1) * P, :], gu_hi[:, c, w], gu_lo[:, c, w]))
            w = slice(u * H, (u + 1) * H)
            loads.append((a["w_dn"][u].rearrange("(c p) n -> p c n", p=P), dn_hi[:, :, w], dn_lo[:, :, w]))

        with nc.sbuf_tensor("e_stage", [P, 4, WC], F32) as stage, nc.Block() as block:
            def staged(n, like):
                s = stage[:, n % 4, :]
                return s.rearrange("p (c n) -> p c n", c=FC) if len(like.shape) == 3 else s

            @block.sync
            def _(sp):
                sp.dma_start(router[:], a["router"].rearrange("(c p) e -> p c e", p=P)).then_inc(small_loaded, 16)
                sp.dma_start(gate[:, 0:1], a["g_ffn"].partition_broadcast(P)).then_inc(small_loaded, 16)
                for n, (src, hi, lo) in enumerate(loads):
                    if n >= 4:
                        sp.wait_ge(w_lo, n - 3)
                    sp.dma_start(staged(n, hi), src).then_inc(w_loaded[n % 4], 16)

            @block.scalar
            def _(act):
                act.wait_ge(small_loaded, 32)
                nc.scalar.activation(gate[:, 1:2], gate[:, 0:1], ACT.Tanh)
                for n, (src, hi, lo) in enumerate(loads):
                    act.wait_ge(w_loaded[n % 4], 16 * (n // 4 + 1))
                    nc.scalar.activation(hi, staged(n, hi), ACT.Copy).then_inc(w_hi, 1)

            @block.vector
            def _(dve):
                for e in range(E):
                    nc.vector.memset(order[:, :, e:e + 1], float(e - E))
                for n, (src, hi, lo) in enumerate(loads):
                    dve.wait_ge(w_hi, n + 1)
                    nc.vector.tensor_tensor(lo, staged(n, hi), hi, ALU.subtract).then_inc(w_lo, 1)

            @block.gpsimd
            def _(pool):
                nc.gpsimd.memset(ident[:], 0.0).then_inc(ident_step, 1)
                pool.wait_ge(ident_step, 1)
                nc.gpsimd.affine_select(out=ident[:], in_=ident[:], compare_op=ALU.not_equal, fill=1.0, base=0,
                                        pattern=[[-1, P]], channel_multiplier=1)

        xs = sb("e_x", [P, 2, TG, H], F32)
        xn = sb("e_xn", [P, TG, H], F32)
        xr = sb("e_xr", [P, TG, H], F32)
        xT_f = sb("e_xT_f", [P, CK, TOK], F32)
        xT_hi = sb("e_xT_hi", [P, 2, CK, TOK], F16)
        xT_lo = sb("e_xT_lo", [P, 2, CK, TOK], F16)
        silu = sb("e_silu", [P, 2, TOK], F32)
        h_f = sb("e_h_f", [P, 2, TOK], F32)
        h_hi = sb("e_h_hi", [P, 2, TOK], F16)
        h_lo = sb("e_h_lo", [P, 2, TOK], F16)
        y = sb("e_y", [P, TG, H], F32)
        stats = sb("e_stats", [P, TG, 6], F32)
        mean = sb("e_mean", [P, TG], F32)
        rstd = sb("e_rstd", [P, TG], F32)
        tmp = sb("e_tmp", [P, 4, TG], F32)
        eps = sb("e_eps", [P, TG], F32)
        top = sb("e_top", [P, TG], F32)
        unused = sb("e_unused", [P, 2], F32)
        first = sb("e_first", [P, TG], F32)
        sig = sb("e_sig", [P, TG], F32)
        cand = sb("e_cand", [P, TG, E], F32)
        score = sb("e_score", [P, TG, E], F32)
        gu = ctx.enter_context(nc.psum_tensor("gu", [P, 2, 2, TOK], F32))
        acc = ctx.enter_context(nc.psum_tensor("acc", [P, TG, H], F32))
        turn = ctx.enter_context(nc.psum_tensor("turn", [P, CK, TOK], F32))

        x_loaded = [sem("e_x0_loaded"), sem("e_x1_loaded")]
        stored = sem("e_stored")
        eps_set = sem("e_eps_set")
        norm_step = sem("e_norm_step")
        turned = sem("e_turned")
        xT_hi_done = sem("e_xT_hi_done")
        xT_done = sem("e_xT_done")
        logits_done = sem("e_logits_done")
        route_step = sem("e_route_step")
        sig_done = sem("e_sig_done")
        xr_done = sem("e_xr_done")
        gu_done = sem("e_gu_done")
        silu_done = sem("e_silu_done")
        h_made = sem("e_h_made")
        h_hi_done = sem("e_h_hi_done")
        h_split = sem("e_h_split")
        down_done = sem("e_down_done")
        acc_full = sem("e_acc_full")
        acc_taken = sem("e_acc_taken")
        CREDIT = 2
        NORM_STEPS = 1 + MOMENT_STEPS + 1
        ROUTE_STEPS = 7

        def experts(fori, chunk):
            for c in range(FC):
                chunk(0, 0, c, False)
            with fori(0, E // 2 - 1) as i:
                for p in (1, 2):
                    for c in range(FC):
                        chunk(i * 2 + p, p % 2, c, False)
            for u in (E - 1, E):
                for c in range(FC):
                    chunk(u, u % 2, c, u == E)

        with nc.Block() as block:
            @block.sync
            def _(sp):
                def load(r, buf):
                    sp.dma_start(xs[:, buf], x1[bass.ds(r * (TG // ST), TG // ST)].rearrange("b (t p) n -> p (b t) n", p=P))\
                        .then_inc(x_loaded[buf], 16)

                load(0, 0)
                for r in range(NG):
                    if r + 1 < NG:
                        if r >= 1:
                            sp.wait_ge(acc_taken, r + 1)
                        load(r + 1, (r + 1) % 2)
                    sp.wait_ge(acc_taken, r + 2)
                    sp.dma_start(out[bass.ds(r * (TG // ST), TG // ST)].rearrange("b (t p) n -> p (b t) n", p=P), y[:])\
                        .then_inc(stored, 16)
                sp.wait_ge(stored, 16 * NG + 16)

            @block.tensor
            def _(pe):
                def gate_up(r, u, parity, c):
                    q = r * CHUNKS + u * FC + c
                    if c == 0:
                        pe.wait_ge(xT_done, r * U + u + 2)
                    pe.wait_ge(h_made, q + (CREDIT - 1))
                    for half in range(2):
                        for i in range(3 * CK):
                            k, part = i // 3, i % 3
                            last = nc.tensor.matmul(
                                gu[:, c % 2, half, :],
                                (gu_hi, gu_lo, gu_hi)[part][:, k, bass.ds(u * (2 * I) + (half * I + c * P), P)],
                                (xT_hi, xT_hi, xT_lo)[part][:, parity, k, :], start=(i == 0), stop=(i == 3 * CK - 1))
                    last.then_inc(gu_done, 1)

                def turn_inputs(r, u, src):
                    pe.wait_ge(xT_done, r * U + u + 1)
                    for t in range(TG):
                        for k in range(CK):
                            last = nc.tensor.transpose(turn[:, k, t * P:(t + 1) * P], src[:, t, k * P:(k + 1) * P], ident[:])
                    last.then_inc(turned, 1)

                def down(r, u, c, final):
                    q = r * CHUNKS + u * FC + c
                    pe.wait_ge(h_split, q + (1 + CREDIT))
                    begin = isinstance(u, int) and u == 0 and c == 0
                    if begin:
                        pe.wait_ge(acc_taken, r + 1)
                    for t in range(TG):
                        for i in range(3):
                            last = nc.tensor.matmul(acc[:, t, :], (h_hi, h_hi, h_lo)[i][:, c % 2, t * P:(t + 1) * P],
                                                    (dn_hi, dn_lo, dn_hi)[i][:, c, bass.ds(u * H, H)],
                                                    start=(begin and i == 0 and t % 2 == 0),
                                                    stop=(final and c == FC - 1 and i == 2), skip_group_check=True)
                    last.then_inc(down_done, 1)

                with pe.Fori(0, NG) as r:
                    pe.wait_ge(norm_step, r * NORM_STEPS + NORM_STEPS)
                    turn_inputs(r, 0, xn)
                    pe.wait_ge(xT_done, r * U + 2)
                    for t in range(TG):
                        for k in range(CK):
                            last = nc.tensor.matmul(turn[:, 0, t * E:(t + 1) * E], xT_f[:, k, t * P:(t + 1) * P], router[:, k, :],
                                                    start=(k == 0), stop=(k == CK - 1))
                    last.then_inc(logits_done, 1)
                    gate_up(r, 0, 0, 0)
                    gate_up(r, 0, 0, 1)

                    def chunk(u, parity, c, final):
                        if c < FC - 2:
                            gate_up(r, u, parity, c + 2)
                        elif not final:
                            gate_up(r, u + 1, 1 - parity, c + 2 - FC)
                        if c == 0 and not final:
                            pe.wait_ge(xr_done, r * E + u + 1)
                            turn_inputs(r, u + 1, xr)
                        down(r, u, c, final)
                    experts(pe.Fori, chunk)
                    nc.tensor.matmul(turn[0:1, 1, 0:1], ident[:, 0:1], ident[:, 0:1], start=True, stop=True).then_inc(acc_full, 1)

            @block.scalar
            def _(act):
                def turned_hi(r, u, parity, keep):
                    act.wait_ge(turned, r * U + u + 1)
                    if keep:
                        nc.scalar.activation(xT_f[:], turn[:], ACT.Copy)
                    nc.scalar.activation(xT_hi[:, parity], turn[:], ACT.Copy).then_inc(xT_hi_done, 1)

                def gate_silu(r, u, c):
                    q = r * CHUNKS + u * FC + c
                    act.wait_ge(gu_done, q + 1)
                    act.wait_ge(h_made, q + (CREDIT - 1))
                    nc.scalar.activation(silu[:, c % 2, :], gu[:, c % 2, 0, :], ACT.Silu).then_inc(silu_done, 1)

                with act.Fori(0, NG) as r:
                    turned_hi(r, 0, 0, True)
                    act.wait_ge(route_step, r * ROUTE_STEPS + 1)
                    nc.scalar.activation(sig[:], top[:], ACT.Tanh, scale=0.5).then_inc(sig_done, 1)
                    gate_silu(r, 0, 0)

                    def chunk(u, parity, c, final):
                        q = r * CHUNKS + u * FC + c
                        act.wait_ge(h_made, q + (1 + CREDIT))
                        act.wait_ge(down_done, q + 1)
                        nc.scalar.activation(h_hi[:, c % 2, :], h_f[:, c % 2, :], ACT.Copy).then_inc(h_hi_done, 1)
                        if c < FC - 1:
                            gate_silu(r, u, c + 1)
                        elif not final:
                            gate_silu(r, u + 1, 0)
                        if c == 0 and not final:
                            turned_hi(r, u + 1, 1 - parity, False)
                    experts(act.Fori, chunk)

            @block.vector
            def _(dve):
                def turned_lo(r, u, parity):
                    dve.wait_ge(xT_hi_done, r * U + u + 1)
                    nc.vector.tensor_tensor(xT_lo[:, parity], turn[:], xT_hi[:, parity], ALU.subtract).then_inc(xT_done, 1)

                def scaled(r, u):
                    dve.wait_ge(turned, r * U + u)
                    s = score[:, :, bass.ds(u - 1, 1)].to_broadcast([P, TG, H])
                    nc.vector.tensor_tensor(xr[:], xn[:], s, ALU.mult).then_inc(xr_done, 1)

                nc.vector.memset(eps[:], EPS).then_inc(h_made, CREDIT)
                nc.vector.memset(top[:], 0.0).then_inc(xT_done, 1)
                nc.vector.memset(first[:], 0.0).then_inc(acc_taken, 1)
                nc.vector.memset(rstd[:], 0.0).then_inc(stored, 16)
                with dve.Fori(0, NG // 2) as r2:
                    for buf in range(2):
                        r = r2 * 2 + buf
                        dve.wait_ge(x_loaded[buf], r2 * 16 + 16)
                        n = [0]

                        def wait(ins):
                            n[0] += 1
                            ins.then_inc(norm_step, 1)
                            dve.wait_ge(norm_step, r * NORM_STEPS + n[0])
                        for t in range(TG):
                            last = nc.vector.bn_stats(stats[:, t, :], xs[:, buf, t, :])
                        wait(last)
                        for _ in moments(nc, stats[:], H, mean[:], rstd[:], [tmp[:, i] for i in range(4)], eps[:], wait):
                            pass
                        for t in range(TG):
                            last = nc.vector.tensor_scalar(xn[:, t, :], xs[:, buf, t, :], mean[:, t:t + 1], rstd[:, t:t + 1],
                                                           ALU.subtract, ALU.mult)
                        wait(last)
                        assert n[0] == NORM_STEPS
                        turned_lo(r, 0, 0)

                        m = [0]

                        def route(ins):
                            m[0] += 1
                            ins.then_inc(route_step, 1)
                            dve.wait_ge(route_step, r * ROUTE_STEPS + m[0])
                        logits = turn[:, 0, 0:TG * E].rearrange("p (t e) -> p t e", e=E)
                        over_e = [P, TG, E]
                        dve.wait_ge(logits_done, r + 1)
                        route(nc.vector.tensor_reduce(top[:], logits, AX_X, ALU.max))
                        route(nc.vector.tensor_tensor(cand[:], logits, top[:].unsqueeze(2).to_broadcast(over_e), ALU.is_equal))
                        route(nc.vector.tensor_tensor(cand[:], cand[:], order[:], ALU.mult))
                        route(nc.vector.tensor_reduce(first[:], cand[:], AX_X, ALU.min))
                        route(nc.vector.tensor_tensor(cand[:], order[:], first[:].unsqueeze(2).to_broadcast(over_e), ALU.is_equal))
                        dve.wait_ge(sig_done, r + 1)
                        route(nc.vector.tensor_scalar(first[:], sig[:], 0.5, 0.5, ALU.mult, ALU.add))
                        route(nc.vector.tensor_tensor(score[:], cand[:], first[:].unsqueeze(2).to_broadcast(over_e), ALU.mult))
                        assert m[0] == ROUTE_STEPS
                        scaled(r, 1)

                        def chunk(u, parity, c, final):
                            q = r * CHUNKS + u * FC + c
                            dve.wait_ge(silu_done, q + 1)
                            dve.wait_ge(h_split, q + 1)
                            nc.vector.tensor_tensor(h_f[:, c % 2, :], silu[:, c % 2, :], gu[:, c % 2, 1, :], ALU.mult)\
                                .then_inc(h_made, 1)
                            if c == 1 and not final:
                                turned_lo(r, u + 1, 1 - parity)
                            if c == 2 and not final and not (isinstance(u, int) and u == E - 1):
                                scaled(r, u + 2)
                        experts(dve.Fori, chunk)
                        dve.wait_ge(acc_full, r + 1)
                        dve.wait_ge(stored, r * 16 + 16)
                        nc.vector.scalar_tensor_tensor(out=y[:], in0=acc[:], scalar=gate[:, 1:2], in1=xs[:, buf], op0=ALU.mult,
                                                       op1=ALU.add).then_inc(acc_taken, 1)

            @block.gpsimd
            def _(pool):
                nc.gpsimd.memset(unused[:, 0:1], 0.0).then_inc(h_split, CREDIT)
                nc.gpsimd.memset(unused[:, 1:2], 0.0).then_inc(down_done, CREDIT)
                with pool.Fori(0, NG) as r:
                    def chunk(u, parity, c, final):
                        q = r * CHUNKS + u * FC + c
                        pool.wait_ge(h_hi_done, q + 1)
                        nc.gpsimd.tensor_tensor(h_lo[:, c % 2, :], h_f[:, c % 2, :], h_hi[:, c % 2, :], ALU.subtract)\
                            .then_inc(h_split, 1)
                    experts(pool.Fori, chunk)


def program(nc, a, out):
    inv_smooth = nc.dram_tensor("inv_smooth", (G, 4 * D), F32, kind="Internal").ap()
    x1 = nc.dram_tensor("x1", (B, S, H), F32, kind="Internal").ap()
    attention_block(nc, a, x1, inv_smooth)
    experts_block(nc, a, x1, out)


_IN_SCALES = ["L0_xattn_q_in_scale", "L0_xattn_k_in_scale", "L0_xattn_v_in_scale", "L0_xattn_qx_in_scale"]


def kernel(**inputs):
    import numpy as np
    import concourse.bacc as bacc
    from concourse.bass_utils import run_bass_kernel_spmd

    def get(name):
        return np.asarray(inputs[name])

    def att(name):
        return get("L0_xattn_" + name)

    def group_rows(w, n):
        return w.reshape(G, n * D, H)

    arrays = {}
    arrays["x"] = get("x")
    arrays["ctxT"] = get("ctx_2048").transpose(0, 2, 1)
    arrays["w_self"] = np.concatenate([group_rows(att("wq"), HPG), group_rows(att("wk"), 1), group_rows(att("wv"), 1),
                                       group_rows(att("wqx"), HPG)], axis=1).reshape(G * GW, H).T
    kv = att("w_kv_x")
    arrays["w_kv"] = np.concatenate([group_rows(kv[:G * D], 1), group_rows(kv[G * D:], 1)], axis=1).reshape(G * 2 * D, H).T
    arrays["w_proj"] = att("wproj").T.reshape(2, G, HPG, D, H).transpose(3, 1, 0, 2, 4).reshape(D, 4 * G, H)
    arrays["smooth"] = att("proj_smooth").reshape(2, G, HPG * D).transpose(1, 0, 2).reshape(G, 4 * D)
    arrays["scales"] = np.stack([get(n) for n in _IN_SCALES])
    arrays["ln_w"], arrays["ln_b"] = att("ln_w"), att("ln_b")
    cols = [get(n).reshape(CK, P)[c] for n in _IN_SCALES for c in range(CK)]
    cols += [att(n) for n in ("qln_w", "qln_b", "kln_w", "kln_b", "qxln_w", "qxln_b", "kxln_w", "kxln_b")]
    cols += [np.broadcast_to(att(n), (P,)) for n in ("wq_scale", "wk_scale", "wqx_scale", "wv_scale", "proj_w_scale", "proj_in_scale")]
    cols += [np.broadcast_to(get("g_xattn"), (P,))]
    arrays["cols"] = np.stack(cols, axis=1)

    ffn = {n: get("L0_ffn_" + n) for n in ("router_w", "gate_up_proj", "down_proj", "shared_gate_w", "shared_up_w", "shared_down_w")}
    arrays["router"] = ffn["router_w"].T
    arrays["w_gu"] = np.concatenate([np.concatenate([ffn["shared_gate_w"], ffn["shared_up_w"]], axis=1)[None], ffn["gate_up_proj"]])
    arrays["w_dn"] = np.concatenate([ffn["shared_down_w"][None], ffn["down_proj"]])
    arrays["g_ffn"] = get("g_ffn")

    nc = bacc.Bacc("TRN2", target_bir_lowering=False, num_devices=1)
    fed, aps = {}, {}
    for name, v in arrays.items():
        v = np.ascontiguousarray(v)
        fed["in_" + name] = v
        aps[name] = nc.dram_tensor("in_" + name, v.shape, mybir.dt.from_np(v.dtype), kind="ExternalInput").ap()
    out = nc.dram_tensor("out", (B, S, H), F32, kind="ExternalOutput").ap()
    program(nc, aps, out)
    return run_bass_kernel_spmd(nc, [fed], core_ids=[0]).results[0]["out"]
```

```python
from contextlib import ExitStack

import concourse.bass as bass
from concourse import mybir

ALU = mybir.AluOpType
ACT = mybir.ActivationFunctionType
AX_X = mybir.AxisListType.X
AX_XY = mybir.AxisListType.XY
F32 = mybir.dt.float32
F16 = mybir.dt.float16
BF16 = mybir.dt.bfloat16
U16 = mybir.dt.uint16
I32 = mybir.dt.int32

P = 128
B, S, H = 8, 256, 256
SC = 1601
G, HPG, D = 8, 2, 128
CK = H // P
ST = S // P
CT = (SC + P - 1) // P
LAST = SC - (CT - 1) * P
NT = ST + CT
Q = HPG * S
GW = 2 * HPG * D + 2 * D
VW = D + 1
SCALE = float(D) ** -0.5
EPS = 1e-5
FP8_MAX = 448.0
E, I = 8, 512
FC = I // P
LEAD = 2
RING = 3

STEP_JOBS = {0: ["SP0", "KV0"], 1: ["SP1", "KV1"], 2: ["KV2", "KV3"], 3: ["KV4", "KV5"], 4: ["KV6", "OT"], 5: ["ST0"],
             6: ["ST1", "KT0"], 7: ["MS0"], 8: ["MS1", "KT1"], 9: ["MX0", "MX1"], 10: ["NS", "MX2", "MX3"],
             11: ["MX4"], 12: ["MX5", "MX6"], 13: ["MX7"], 14: ["NC"]}
ROUND_JOBS = {12: ["XA0"], 13: ["XA1"]}
OUTPUT_JOBS = {5: ["PJ0"], 6: ["PJ1"]}
PREP_JOBS = 25
ROW_JOBS = G * (PREP_JOBS + 1) + 4
KV_TILES = [(2 * j, 2) for j in range(CT // 2)] + [(CT - 1, 1)]
KT_TILES = [(0, 8), (8, 5)]
MX_STARTS = [0, 400, 800, SC - 401]
MX_W = 401


def rows_of(t):
    return LAST if t == CT - 1 else P


def body_jobs(attend, prep, ot, phase_a, pj):
    steps = []
    for k in range(NT):
        names = [n for n in STEP_JOBS.get(k, []) if (ot if n == "OT" else prep)]
        if phase_a:
            names += ROUND_JOBS.get(k, [])
        if pj:
            names += OUTPUT_JOBS.get(k, [])
        steps.append(names)
    return steps


class Jobs:

    def __init__(self, half, const):
        self.half, self.const = half, const

    def slot(self):
        return self.const % 2

    def released_before(self):
        return self.half + self.const // 2

    def ready(self):
        return self.half * 2 + (self.const + 1)

    def back(self, n):
        return Jobs(self.half, self.const - n)

    def step(self):
        self.const += 1


def plan(engine, fori):
    every = PREP_JOBS + 1
    engine.body(-1, G - 1, Jobs(0, 0), attend=False, phase_a=True, new_row=True, ot=False)
    at = PREP_JOBS + 2
    engine.body(0, 0, Jobs(0, at), ot=False)
    at += PREP_JOBS

    def rest(b, last):
        half = b * (ROW_JOBS // 2)
        engine.body(b, 1, Jobs(half, at))
        with fori(0, 2) as i:
            engine.body(b, i * 2 + 2, Jobs(half + i * every, at + every), parity=0, pair=i + 1)
            engine.body(b, i * 2 + 3, Jobs(half + i * every, at + 2 * every), parity=1, pair=i + 1)
        engine.body(b, 6, Jobs(half, at + 5 * every), phase_a=not last)
        engine.body(b, 7, Jobs(half, at + 6 * every + (0 if last else 2)), prep=not last, new_row=not last)
        return half, at + 7 * every + (0 if last else 2)

    with fori(0, B - 1) as b:
        half, n = rest(b, False)
        engine.body(b + 1, 0, Jobs(half, n), pj=True)
    half, n = rest(B - 1, True)
    engine.tail(B - 1, Jobs(half, n - PREP_JOBS))


NEWTON = 3
RSQRT_STEPS = 1 + 3 * NEWTON


def rsqrt(nc, out, v, t, wait):
    yield wait(nc.vector.tensor_scalar(out.bitcast(I32), v.bitcast(I32), -0.5, float(0x5F3759DF), ALU.mult, ALU.add))
    for _ in range(NEWTON):
        yield wait(nc.vector.tensor_tensor(t, out, out, ALU.mult))
        yield wait(nc.vector.scalar_tensor_tensor(out=t, in0=t, scalar=-0.5, in1=v, op0=ALU.mult, op1=ALU.mult))
        yield wait(nc.vector.scalar_tensor_tensor(out=out, in0=t, scalar=1.5, in1=out, op0=ALU.add, op1=ALU.mult))


MOMENT_STEPS = 4 + RSQRT_STEPS


def moments(nc, stats, n, mean, rstd, tmp, eps, wait):
    me, mo, ve, vo = (stats[:, :, i] for i in (1, 4, 2, 5))
    nc.vector.tensor_tensor(tmp[0], me, mo, ALU.add)
    nc.vector.tensor_tensor(tmp[1], me, mo, ALU.subtract)
    yield wait(nc.vector.tensor_tensor(tmp[2], ve, vo, ALU.add))
    nc.vector.tensor_scalar(mean, tmp[0], 0.5, None, ALU.mult)
    yield wait(nc.vector.scalar_tensor_tensor(out=tmp[3], in0=tmp[1], scalar=0.25, in1=tmp[1], op0=ALU.mult, op1=ALU.mult))
    yield wait(nc.vector.scalar_tensor_tensor(out=tmp[3], in0=tmp[2], scalar=1.0 / n, in1=tmp[3], op0=ALU.mult, op1=ALU.add))
    yield wait(nc.vector.tensor_tensor(tmp[3], tmp[3], eps, ALU.add))
    yield from rsqrt(nc, rstd, tmp[3], tmp[2], wait)


def attention_block(nc, a, x1_dram, inv_smooth):
    with ExitStack() as ctx:
        def sb(name, shape, dt):
            return ctx.enter_context(nc.sbuf_tensor(name, shape, dt))

        def sem(name):
            return ctx.enter_context(nc.semaphore(name))

        ident32 = sb("ident32", [P, P], F32)
        ident16 = sb("ident16", [P, P], F16)
        identb = sb("identb", [P, P], BF16)
        ones_row = sb("ones_row", [1, P], BF16)
        w_self = sb("w_self", [P, CK, G * GW], F16)
        wkv_hi = sb("wkv_hi", [P, CK, G * 2 * D], F16)
        wkv_lo = sb("wkv_lo", [P, CK, G * 2 * D], F16)
        w_proj = sb("w_proj", [P, 4 * G, H], F16)
        cols = sb("cols", [P, 32], F32)
        inv_scale = sb("inv_scale", [P, 4, H], F32)
        lnw_bc = sb("lnw_bc", [P, H], F32)
        lnb_bc = sb("lnb_bc", [P, H], F32)
        eps_w = sb("eps_w", [P, 10 + CT], F32)
        COL = {"in_scale": 0, "qw": 8, "qb": 9, "kw": 10, "kb": 11, "xw": 12, "xb": 13, "cw": 14, "cb": 15,
               "wq_s": 16, "wk_s": 17, "wx_s": 18, "wv_s": 19, "pw_s": 20, "pin_s": 21, "gate": 22, "coef": 23,
               "e0": 24}

        def col(name, i=0, rows=P):
            return cols[0:rows, COL[name] + i:COL[name] + i + 1]

        w_loaded = [sem(f"w{i}_loaded") for i in range(4)]
        small_loaded = sem("small_loaded")
        w_part = sem("w_part")
        w_center_step = sem("w_center_step")
        w_centered = sem("w_centered")
        smooth_in_loaded = sem("smooth_in_loaded")
        smooth_inverted = sem("smooth_inverted")
        inv_stored = sem("inv_stored")
        w_hi = sem("w_hi")
        w_lo = sem("w_lo")
        zeroed = sem("zeroed")
        ident_made = sem("ident_made")
        eps_step = sem("eps_step")
        coef_step = sem("coef_step")

        WC = 2048
        loads = []
        for c in range(CK):
            for n in range(G * GW // WC):
                loads.append((a["w_self"][c * P:(c + 1) * P, n * WC:(n + 1) * WC], w_self[:, c, n * WC:(n + 1) * WC], None))
            loads.append((a["w_kv"][c * P:(c + 1) * P, :], wkv_hi[:, c, :], wkv_lo[:, c, :]))
        for n in range(4):
            w = 4 * G // 4
            loads.append((a["w_proj"][:, n * w:(n + 1) * w, :].rearrange("p c n -> p (c n)"),
                          w_proj[:, n * w:(n + 1) * w, :].rearrange("p c n -> p (c n)"), None))
        with nc.sbuf_tensor("w_stage", [P, 4, WC], F32) as w_stage, \
                nc.sbuf_tensor("w_mean", [P, 2, G], F32) as w_mean, nc.sbuf_tensor("scale_in", [P, 4, H], F32) as scale_in, \
                nc.sbuf_tensor("smooth_in", [P, 2, G * 4 * D // P], F32) as smooth_in, nc.Block() as block:
            @block.sync
            def _(sp):
                spread = "g (q n) -> (g q) n"
                sp.dma_start(smooth_in[:, 0], a["smooth"].rearrange(spread, n=G * 4 * D // P)).then_inc(smooth_in_loaded, 16)
                sp.wait_ge(smooth_inverted, 1)
                sp.dma_start(inv_smooth.rearrange(spread, n=G * 4 * D // P), smooth_in[:, 1]).then_inc(inv_stored, 16)
                for src, dst in ((a["cols"], cols[:, 0:COL["coef"]]),
                                 (a["scales"].partition_broadcast(P), scale_in[:]),
                                 (a["ln_w"].partition_broadcast(P), lnw_bc[:]),
                                 (a["ln_b"].partition_broadcast(P), lnb_bc[:])):
                    sp.dma_start(dst, src).then_inc(small_loaded, 16)
                for n, (src, hi, lo) in enumerate(loads):
                    if n >= 4:
                        sp.wait_ge(w_part, n - 3)
                    sp.dma_start(w_stage[:, n % 4, :], src).then_inc(w_loaded[n % 4], 16)
                sp.wait_ge(inv_stored, 16)

            @block.scalar
            def _(act):
                seen = 0
                for n, (src, hi, lo) in enumerate(loads):
                    if lo is None:
                        continue
                    seen += 1
                    act.wait_ge(w_centered, seen)
                    nc.scalar.activation(hi, w_stage[:, n % 4, :], ACT.Copy).then_inc(w_hi, 1)
                act.wait_ge(small_loaded, 64)
                nc.scalar.activation(col("coef"), col("gate"), ACT.Tanh).then_inc(coef_step, 1)

            @block.vector
            def _(dve):
                dve.wait_ge(smooth_in_loaded, 16)
                nc.vector.reciprocal(smooth_in[:, 1], smooth_in[:, 0]).then_inc(smooth_inverted, 1)
                seen_hi = 0
                for n, (src, hi, lo) in enumerate(loads):
                    dve.wait_ge(w_loaded[n % 4], 16 * (n // 4 + 1))
                    if lo is None:
                        nc.vector.tensor_copy(hi, w_stage[:, n % 4, :]).then_inc(w_part, 1)
                    else:
                        seen_hi += 1
                        k_cols = w_stage[:, n % 4, :].rearrange("p (g s n) -> p g s n", s=2, n=D)[:, :, 0, :]
                        nc.vector.tensor_reduce(w_mean[:, 0, :], k_cols, AX_X, ALU.add).then_inc(w_center_step, 1)
                        dve.wait_ge(w_center_step, seen_hi * 2 - 1)
                        nc.vector.tensor_scalar(w_mean[:, 1, :], w_mean[:, 0, :], 1.0 / D, None, ALU.mult).then_inc(w_center_step, 1)
                        dve.wait_ge(w_center_step, seen_hi * 2)
                        nc.vector.tensor_tensor(k_cols, k_cols, w_mean[:, 1, :].unsqueeze(2).to_broadcast([P, G, D]), ALU.subtract)\
                            .then_inc(w_centered, 1)
                        dve.wait_ge(w_hi, seen_hi)
                        nc.vector.tensor_tensor(lo, w_stage[:, n % 4, :], hi, ALU.subtract).then_inc(w_part, 1)
                dve.wait_ge(small_loaded, 64)
                nc.vector.reciprocal(inv_scale[:], scale_in[:])
                nc.vector.tensor_tensor(cols[:, 24:27], cols[:, 16:19], cols[:, 16:19], ALU.mult).then_inc(eps_step, 1)
                dve.wait_ge(eps_step, 1)
                nc.vector.reciprocal(cols[:, 27:30], cols[:, 24:27]).then_inc(eps_step, 1)
                nc.vector.memset(eps_w[:], EPS).then_inc(eps_step, 1)
                dve.wait_ge(eps_step, 3)
                for i in range(10):
                    w = [0, 0, 1, 2, 2][i % 5]
                    last = nc.vector.tensor_scalar(eps_w[:, i:i + 1], cols[:, 27 + w:28 + w], EPS, None, ALU.mult)
                dve.wait_ge(coef_step, 1)
                nc.vector.scalar_tensor_tensor(out=cols[:, 30:31], in0=col("pw_s"), scalar=col("pin_s"), in1=col("coef"),
                                               op0=ALU.mult, op1=ALU.mult).then_inc(coef_step, 1)

            @block.gpsimd
            def _(pool):
                nc.gpsimd.memset(ident32[:], 0.0).then_inc(zeroed, 1)
                nc.gpsimd.memset(ones_row[:], 1.0).then_inc(zeroed, 1)
                pool.wait_ge(zeroed, 2)
                nc.gpsimd.affine_select(out=ident32[:], in_=ident32[:], compare_op=ALU.not_equal, fill=1.0, base=0,
                                        pattern=[[-1, P]], channel_multiplier=1).then_inc(ident_made, 1)
                pool.wait_ge(ident_made, 1)
                nc.gpsimd.tensor_copy(ident16[:], ident32[:]).then_inc(ident_made, 1)
                nc.gpsimd.tensor_copy(identb[:], ident32[:]).then_inc(ident_made, 1)
        COL["coef"] = 30

        catT = sb("catT", [P, 4 * G, S], F16)
        ctx_in = sb("ctx_in", [P, SC], F32)
        ctx_hi = sb("ctx_hi", [P, CK, SC], F16)
        ctx_lo = sb("ctx_lo", [P, CK, SC], F16)
        xq_hi = sb("xq_hi", [P, 4, CK, S], F16)
        xq_lo = sb("xq_lo", [P, 4, CK, S], F16)
        xt = sb("xt", [P, ST, H], F32)
        x_res = sb("x_res", [P, ST, H], F32)
        x_stats = sb("x_stats", [P, ST, 6], F32)
        x_mean = sb("x_mean", [P, ST], F32)
        eps_x = sb("eps_x", [P, ST], F32)
        x_rstd = sb("x_rstd", [P, ST], F32)
        x_tmp = sb("x_tmp", [P, 4, ST], F32)
        smooth = sb("smooth", [P, 2, 4 * D], F32)
        yo = sb("yo", [P, 1024], BF16)
        q_mag = sb("q_mag", [P, 1024], BF16)
        q_sum = sb("q_sum", [P, 1024], F32)
        rq = sb("rq", [P, ST, 1024], BF16)
        ro = sb("ro", [P, 1024], BF16)
        raw_self = sb("raw_self", [P, ST, GW], F32)
        raw_k = sb("raw_k", [P, CT, D], F32)
        stats = sb("stats", [P, 10 + CT, 6], F32)
        st_a = sb("st_a", [P, 10 + CT], F32)
        st_b = sb("st_b", [P, 10 + CT], F32)
        st_c = sb("st_c", [P, 10 + CT], F32)
        st_d = sb("st_d", [P, 10 + CT], F32)
        mean = sb("mean", [P, 10 + CT], F32)
        rstd = sb("rstd", [P, 10 + CT], F32)
        norm_bias = sb("norm_bias", [P, 5], F32)
        selfT_f = sb("selfT_f", [P, 5, S], F32)
        kxT_f = sb("kxT_f", [P, SC], F32)
        selfT_hi = sb("selfT_hi", [P, 2, 5, S], F16)
        selfT_lo = sb("selfT_lo", [P, 2, 5, S], F16)
        kxT_hi = sb("kxT_hi", [P, 2, SC], F16)
        kxT_lo = sb("kxT_lo", [P, 2, SC], F16)
        v_hi = sb("v_hi", [P, 2, NT, VW], F16)
        v_lo = sb("v_lo", [P, 2, NT, D], F16)
        neg_max = sb("neg_max", [1, 2, 2 * Q], BF16)
        mx = sb("mx", [P, 2, 8], F32)
        mx_neg = sb("mx_neg", [P, 8], BF16)
        p_f = sb("p_f", [P, RING, Q], F32)
        p_hi = sb("p_hi", [P, RING, Q], F16)
        p_lo = sb("p_lo", [P, RING, Q], F16)
        o_rinv = sb("o_rinv", [P, 2, 4], F32)
        score = ctx.enter_context(nc.psum_tensor("score", [P, 2, 512], F32))
        o_ps = ctx.enter_context(nc.psum_tensor("o_ps", [P, 2, 512], F32))
        work = ctx.enter_context(nc.psum_tensor("work", [P, 2, 1024], F32))

        work_ready = sem("work_ready")
        slot_free = [sem("slot0_free"), sem("slot1_free")]
        x_loaded = sem("x_loaded")
        ctx_loaded = sem("ctx_loaded")
        smooth_loaded = [sem("smooth0_loaded"), sem("smooth1_loaded")]
        xres_loaded = sem("xres_loaded")
        x1_stored = sem("x1_stored")
        x_step = sem("x_step")
        xq_hi_done = sem("xq_hi_done")
        ctx_hi_done = sem("ctx_hi_done")
        ctx_split = sem("ctx_split")
        vself_hi_done = sem("vself_hi_done")
        kv_evac = sem("kv_evac")
        stat_step = sem("stat_step")
        self_norm = [sem("self_norm0"), sem("self_norm1")]
        norm_bias_done = sem("norm_bias_done")
        k_norm = sem("k_norm")
        selfT_hi_done = sem("selfT_hi_done")
        kxT_hi_done = sem("kxT_hi_done")
        selfT_lo_done = sem("selfT_lo_done")
        kxT_lo_done = sem("kxT_lo_done")
        mx_done = sem("mx_done")
        mx_step = sem("mx_step")
        scores_done = sem("scores_done")
        exp_done = sem("exp_done")
        plo_dve = sem("plo_dve")
        plo_pool = sem("plo_pool")
        p_free = sem("p_free")
        o_recip = sem("o_recip")
        o_free = sem("o_free")
        q_step = sem("q_step")
        rq_step = sem("rq_step")
        ro_mag = sem("ro_mag")
        ro_sum = sem("ro_sum")
        ro_done = sem("ro_done")
        rq_mag = sem("rq_mag")
        rq_sum = sem("rq_sum")
        rq_done = sem("rq_done")
        init_done = sem("init_done")

        EXP_CREDIT = 2
        CTX_HI_STEPS, CTX_LO_STEPS = (6, 10), (7, 11)
        DVE_LO = 8
        POOL_LO = NT - DVE_LO

        def released(jobs):
            return slot_free[jobs.slot()], jobs.released_before() + 1

        def parity_of(g, parity):
            return g % 2 if parity is None else parity

        class Body:

            def index(self, b, g, parity, pair):
                self.b, self.g = b, g
                self.at = b * G + g if not isinstance(b, int) or b >= 0 else None
                self.pr = b * G + g + 1 if self.at is not None else 0
                self.ap = parity_of(g, parity)
                self.pp = 1 - self.ap
                self.pair = b * (G // 2) + (g // 2 if pair is None else pair)

        def order(steps, attend, phase_a):
            if attend or not phase_a:
                return steps
            return [sum(ROUND_JOBS.values(), [])] + [[n for n in names if n[:2] != "XA"] for names in steps]

        class PE(Body):
            def __init__(self, pe):
                self.pe, self.seen = pe, {}

            def start(self, jobs):
                if not (isinstance(jobs.half, int) and jobs.released_before() == 0):
                    self.pe.wait_ge(slot_free[jobs.slot()], jobs.released_before())
                return work[:, jobs.slot(), :]

            def job(self, name, jobs):
                pe, w = self.pe, self.start(jobs)
                j = int(name[2:]) if name[2:] else 0
                kind, pp = name[:2], self.pp
                if kind == "XA":
                    pe.wait_ge(rq_done, (self.b + 1) * ST + ST)
                    wb = w[:, 0:512].bitcast(BF16).rearrange("p (n s) -> p n s", s=S)
                    for st in range(ST):
                        for n in range(4):
                            o = slice((j * 4 + n) * P, (j * 4 + n + 1) * P)
                            last = nc.tensor.transpose(wb[:, n, st * P:(st + 1) * P], rq[:, st, o], identb[:])
                elif kind == "SP":
                    if j == 0 and self.new_row:
                        pe.wait_ge(*self.seen["XA1"])
                    for lo_col, n, t in ((0, 2 * D, 0), (2 * D, D, 1), (3 * D, D, 2), (4 * D, 2 * D, 3)):
                        for i in range(2 * CK):
                            src = (xq_hi, xq_lo)[i % 2]
                            last = nc.tensor.matmul(w[:, lo_col:lo_col + n], src[:, t, i // 2, j * P:(j + 1) * P],
                                                    w_self[:, i // 2, bass.ds(self.wg * GW + lo_col, n)],
                                                    start=(i == 0), stop=(i == 2 * CK - 1))
                elif kind == "KV":
                    pe.wait_ge(ctx_split, (self.row + 1) * CK)
                    t0, n = KV_TILES[j]
                    for t in range(t0, t0 + n):
                        r = rows_of(t)
                        o = w[0:r, (t - t0) * 2 * D:(t - t0 + 1) * 2 * D]
                        for i in range(3 * CK):
                            c, part = i // 3, i % 3
                            last = nc.tensor.matmul(o, (ctx_hi, ctx_hi, ctx_lo)[part][:, c, t * P:t * P + r],
                                                    (wkv_hi, wkv_lo, wkv_hi)[part][:, c, bass.ds(self.wg * 2 * D, 2 * D)],
                                                    start=(i == 0), stop=(i == 3 * CK - 1))
                elif kind == "ST":
                    pe.wait_ge(self_norm[j], self.pr + 1)
                    for i, c in enumerate((0, 1, 2, 4, 5)):
                        last = nc.tensor.transpose(w[:, i * P:(i + 1) * P], raw_self[:, j, c * P:(c + 1) * P], ident32[:])
                elif kind == "KT":
                    t0, n = KT_TILES[j]
                    pe.wait_ge(k_norm, self.pr * 2 + (j + 1))
                    for t in range(t0, t0 + n):
                        r = rows_of(t)
                        last = nc.tensor.transpose(w[:, (t - t0) * P:(t - t0) * P + r], raw_k[0:r, t, :], ident32[0:r, 0:r])
                elif kind == "MX":
                    if j == 0:
                        pe.wait_ge(kxT_hi_done, self.pr * 2 + 2)
                    q = selfT_hi[:, pp, 3 + j // 4, ((j // 2) % 2) * P:((j // 2) % 2 + 1) * P]
                    for i in range(2):
                        c0 = MX_STARTS[(j % 2) * 2 + i]
                        last = nc.tensor.matmul(w[:, i * 512:i * 512 + MX_W], q, kxT_hi[:, pp, c0:c0 + MX_W], start=True, stop=True)
                elif kind == "MS":
                    if j == 0:
                        pe.wait_ge(selfT_hi_done, self.pr * ST + 2)
                    for st in range(ST):
                        last = nc.tensor.matmul(w[:, st * S:(st + 1) * S], selfT_hi[:, pp, j, st * P:(st + 1) * P],
                                                selfT_hi[:, pp, 2, :], start=True, stop=True)
                elif kind in ("NS", "NC"):
                    context = int(kind == "NC")
                    pe.wait_ge(mx_step, self.pr * 2 + (1 + context))
                    for i in range(4):
                        last = nc.tensor.matmul(w[0:1, i * P:(i + 1) * P], mx_neg[:, context * 4 + i:context * 4 + i + 1],
                                                identb[:], start=True, stop=True)
                elif kind == "OT":
                    pe.wait_ge(ro_done, self.ot)
                    wb = w.bitcast(BF16)
                    for i in range(8):
                        last = nc.tensor.transpose(wb[:, i * P:(i + 1) * P], ro[:, i * P:(i + 1) * P], identb[:])
                elif kind == "PJ":
                    if j == 0:
                        pe.wait_ge(*self.seen["OT0"])
                    for c in range(4 * G):
                        last = nc.tensor.matmul(w[:, 0:H], catT[:, c, j * P:(j + 1) * P], w_proj[:, c, :],
                                                start=(c == 0), stop=(c == 4 * G - 1))
                last.then_inc(work_ready, 1)
                self.seen[name if name[2:] else name + "0"] = released(jobs)
                jobs.step()

            def scores(self, k, ahead=0):
                pe, ap = self.pe, (self.pp if ahead else self.ap)
                a_ = self.pr if ahead else self.at
                t = k - ST
                r = P if k < ST else rows_of(t)
                tile = a_ * NT + k
                if k == 0:
                    pe.wait_ge(*self.seen["NS0"])
                    pe.wait_ge(selfT_lo_done, a_ * ST + 3)
                if k == ST:
                    pe.wait_ge(*released(self.nc_job))
                    pe.wait_ge(kxT_lo_done, a_ * 2 + 3)
                pe.wait_ge(exp_done, tile + 1)
                q = slice(0, 2) if k < ST else slice(3, 5)
                q_hi = selfT_hi[:, ap, q, :].rearrange("p h s -> p (h s)")
                q_lo = selfT_lo[:, ap, q, :].rearrange("p h s -> p (h s)")
                if k < ST:
                    k_hi, k_lo = (x[:, ap, 2, k * P:(k + 1) * P] for x in (selfT_hi, selfT_lo))
                else:
                    k_hi, k_lo = (x[:, ap, t * P:t * P + r] for x in (kxT_hi, kxT_lo))
                o = score[0:r, (ap + k) % 2, :]
                nc.tensor.matmul(o, k_hi, q_hi, start=True, stop=False)
                nc.tensor.matmul(o, k_hi, q_lo, start=False, stop=False)
                nc.tensor.matmul(o, k_lo, q_hi, start=False, stop=False)
                at = 0 if k < ST else Q
                nc.tensor.matmul(o, ones_row[:, 0:r], neg_max[:, ap, at:at + Q], start=False, stop=True).then_inc(scores_done, 1)

            def pv(self, k):
                pe, ap, a_ = self.pe, self.ap, self.at
                t = k - ST
                r = P if k < ST else rows_of(t)
                if k == 0:
                    pe.wait_ge(o_free, a_ * 2 + 1)
                if k == ST:
                    pe.wait_ge(o_free, a_ * 2 + 2)
                if k % 2 == 0:
                    pe.wait_ge(plo_dve, a_ * DVE_LO + (k // 2 + 1))
                else:
                    pe.wait_ge(plo_pool, a_ * POOL_LO + (k // 2 + 1))
                first, final = k in (0, ST), k in (ST - 1, NT - 1)
                for j in range(4):
                    o = o_ps[:, j // 3, (j % 3) * VW:(j % 3) * VW + VW]
                    ph = p_hi[0:r, k % RING, j * P:(j + 1) * P]
                    pl = p_lo[0:r, k % RING, j * P:(j + 1) * P]
                    nc.tensor.matmul(o, ph, v_hi[0:r, ap, k, :], start=first and j in (0, 3), stop=False, skip_group_check=True)
                    nc.tensor.matmul(o[:, 0:D], ph, v_lo[0:r, ap, k, :], start=False, stop=False, skip_group_check=True)
                    last = nc.tensor.matmul(o, pl, v_hi[0:r, ap, k, :], start=False, stop=final, skip_group_check=True)
                last.then_inc(p_free, 1)

            def body(self, b, g, jobs, attend=True, prep=True, ot=True, phase_a=False, new_row=False, pj=False, parity=None, pair=None):
                self.index(b, g, parity, pair)
                self.row = b + 1 if new_row else b
                self.new_row = new_row
                self.wg = 0 if new_row else g + 1
                self.ot = self.at
                self.nc_job = jobs.back(1)
                steps = order(body_jobs(attend, prep, ot, phase_a, pj), attend, phase_a)
                for k, names in enumerate(steps):
                    if attend and k + LEAD < NT:
                        self.scores(k + LEAD)
                    if prep and k + LEAD >= NT and len(steps) == NT:
                        self.scores(k + LEAD - NT, 1)
                    for name in names:
                        self.job(name, jobs)
                    if attend:
                        self.pv(k)
                if not attend:
                    for k in range(LEAD):
                        self.scores(k, 1)

            def tail(self, b, jobs):
                self.ot = b * G + G
                for name in ("OT", "PJ0", "PJ1"):
                    self.job(name, jobs)

        class ACTE(Body):
            def __init__(self, act):
                self.act = act

            def job(self, name, jobs):
                act, w, pp = self.act, work[:, jobs.slot(), :], self.pp
                j = int(name[2:]) if name[2:] else 0
                kind = name[:2]
                free = slot_free[jobs.slot()]
                if kind not in ("MX", "MS", "PJ"):
                    act.wait_ge(work_ready, jobs.ready())
                if kind == "XA":
                    wb = w[:, 0:512].bitcast(BF16).rearrange("p (n s) -> p n s", s=S)
                    for i in range(4):
                        n = j * 4 + i
                        last = nc.scalar.activation(xq_hi[:, n // CK, n % CK, :], wb[:, i, :], ACT.Copy, scale=col("in_scale", n))
                    last.then_inc(xq_hi_done, 1)
                elif kind == "SP":
                    nc.scalar.activation(raw_self[:, j, :], w[:, 0:GW], ACT.Copy)
                    nc.scalar.activation(v_hi[:, pp, j, 0:D], w[:, 3 * D:4 * D], ACT.Copy, scale=col("wv_s"))\
                        .then_inc(vself_hi_done, 1)
                elif kind == "KV":
                    t0, n = KV_TILES[j]
                    r = rows_of(t0)
                    o = w[0:r, 0:n * 2 * D].rearrange("p (t n) -> p t n", n=2 * D)
                    nc.scalar.activation(raw_k[0:r, t0:t0 + n, :], o[:, :, 0:D], ACT.Copy)
                    nc.scalar.activation(v_hi[0:r, pp, ST + t0:ST + t0 + n, 0:D], o[:, :, D:2 * D], ACT.Copy).then_inc(kv_evac, 1)
                    if j == len(KV_TILES) - 1:
                        act.wait_ge(norm_bias_done, self.pr + 1)
                        for i, c in enumerate((0, 1, 2, 4, 5)):
                            o = raw_self[:, 1, c * P:(c + 1) * P]
                            last = nc.scalar.activation(o, o, ACT.Identity, bias=norm_bias[:, i:i + 1], scale=rstd[:, 5 + i:6 + i])
                        last.then_inc(self_norm[1], 1)
                elif kind == "ST":
                    if j == 0:
                        act.wait_ge(selfT_lo_done, self.pr * ST + 1)
                    for o, n, wb in ((0, 2, "q"), (2, 1, "k"), (3, 2, "x")):
                        last = nc.scalar.activation(selfT_f[:, o:o + n, j * P:(j + 1) * P],
                                                    w[:, o * P:(o + n) * P].rearrange("p (h s) -> p h s", s=P),
                                                    ACT.Identity, bias=col(wb + "b"), scale=col(wb + "w"))
                    last.then_inc(free, 1)
                elif kind == "KT":
                    if j == 0:
                        act.wait_ge(kxT_lo_done, self.pr * 2 + 1)
                    c0 = KT_TILES[j][0] * P
                    n = min(SC - c0, KT_TILES[j][1] * P)
                    nc.scalar.activation(kxT_f[:, c0:c0 + n], w[:, 0:n], ACT.Identity, bias=col("cb"), scale=col("cw"))\
                        .then_inc(free, 1)
                elif kind in ("NS", "NC"):
                    at = Q if kind == "NC" else 0
                    nc.scalar.activation(neg_max[:, pp, at:at + Q], w[0:1, 0:Q], ACT.Copy).then_inc(free, 1)
                elif kind == "OT":
                    self.out_turned(w, free)
                jobs.step()

            def split_ctx(self, c):
                self.act.wait_ge(ctx_loaded, self.b * (16 * CK) + 16 * (CK + c + 1))
                nc.scalar.activation(ctx_hi[:, c, :], ctx_in[:], ACT.Copy).then_inc(ctx_hi_done, 1)

            def out_turned(self, w, free):
                g = self.cat_g
                nc.scalar.activation(catT[:, bass.ds(g * 4, 4), :].rearrange("p c s -> p (c s)"), w.bitcast(BF16)[:, 0:1024],
                                     ACT.Copy).then_inc(free, 1)

            def exp(self, k, ahead=0):
                act, a_ = self.act, (self.pr if ahead else self.at)
                ap = self.pp if ahead else self.ap
                r = P if k < ST else rows_of(k - ST)
                tile = a_ * NT + k
                act.wait_ge(scores_done, tile + 1)
                act.wait_ge(p_free, tile + 1)
                s = score[0:r, (ap + k) % 2, :]
                nc.scalar.activation(p_f[0:r, k % RING, :], s, ACT.Exp, scale=SCALE)
                nc.scalar.activation(p_hi[0:r, k % RING, :], s, ACT.Exp, scale=SCALE).then_inc(exp_done, 1)

            def body(self, b, g, jobs, attend=True, prep=True, ot=True, phase_a=False, new_row=False, pj=False, parity=None, pair=None):
                self.index(b, g, parity, pair)
                self.cat_g = G - 1 if pj else g - 1
                steps = order(body_jobs(attend, prep, ot, phase_a, pj), attend, phase_a)
                if not attend:
                    for c in range(CK):
                        self.split_ctx(c)
                for k, names in enumerate(steps):
                    if attend and k + 1 < NT:
                        self.exp(k + 1)
                    if attend and prep and k + 1 == NT:
                        self.exp(0, 1)
                    for name in names:
                        self.job(name, jobs)
                    if attend and phase_a and k in CTX_HI_STEPS:
                        self.split_ctx(CTX_HI_STEPS.index(k))
                if not attend:
                    self.exp(0, 1)

            def tail(self, b, jobs):
                self.cat_g = G - 1
                self.job("OT", jobs)
                jobs.step()
                jobs.step()

        X_STEPS = 2 * (2 + MOMENT_STEPS) + 2 + ST
        NORM_JOBS = (3, 4)
        Q_STEPS = 2
        MAG_STEPS = (3, 9)
        STAT_STEPS = 2 * (1 + MOMENT_STEPS)
        class DVE(Body):
            def __init__(self, dve):
                self.dve = dve

            def magnitudes(self, y, wait):
                wait(nc.vector.tensor_scalar(y, y, FP8_MAX, -FP8_MAX, ALU.min, ALU.max))
                wait(nc.vector.tensor_scalar(q_mag[:].bitcast(U16), y.bitcast(U16), 0x7F80, 0x0040,
                                             ALU.bitwise_and, ALU.bitwise_or))
                return nc.vector.tensor_scalar(q_mag[:], q_mag[:], 1.5 * 2.0 ** -6, 2.0 ** 20, ALU.max, ALU.mult)

            def norm_tokens(self):
                dve, base = self.dve, (self.b + 1) * X_STEPS
                dve.wait_ge(x_loaded, (self.b + 1) * 16 + 16)
                n = [0]

                def wait(ins):
                    n[0] += 1
                    ins.then_inc(x_step, 1)
                    dve.wait_ge(x_step, base + n[0])

                for rnd in range(2):
                    for st in range(ST):
                        last = nc.vector.bn_stats(x_stats[:, st, :], xt[:, st, :])
                    wait(last)
                    for i, _ in enumerate(moments(nc, x_stats[:], H, x_mean[:], x_rstd[:], [x_tmp[:, i] for i in range(4)],
                                                  eps_x[:], wait)):
                        if i % 5 == 4:
                            yield
                    for st in range(ST):
                        last = nc.vector.tensor_scalar(xt[:, st, :], xt[:, st, :], x_mean[:, st:st + 1], x_rstd[:, st:st + 1],
                                                       ALU.subtract, ALU.mult)
                    wait(last)
                    yield
                wait(nc.vector.tensor_tensor(xt[:], xt[:], lnw_bc[:].unsqueeze(1).to_broadcast([P, ST, H]), ALU.mult))
                yield
                wait(nc.vector.tensor_tensor(xt[:], xt[:], lnb_bc[:].unsqueeze(1).to_broadcast([P, ST, H]), ALU.add))
                for st in range(ST):
                    yield
                    wait(nc.vector.tensor_tensor(rq[:, st, :].rearrange("p (t n) -> p t n", t=4),
                                                 xt[:, st, :].unsqueeze(1).to_broadcast([P, 4, H]), inv_scale[:], ALU.mult))
                assert n[0] == X_STEPS

            def token_magnitudes(self, st):
                dve, base, n = self.dve, (self.b + 1) * (2 * ST) + 2 * st, [0]
                if not (isinstance(self.b, int) and self.b < 0 and st == 0):
                    dve.wait_ge(rq_done, (self.b + 1) * ST + st)
                if self.at is not None and st == 0:
                    dve.wait_ge(ro_done, self.at)

                def wait(ins):
                    n[0] += 1
                    ins.then_inc(rq_step, 1)
                    dve.wait_ge(rq_step, base + n[0])
                self.magnitudes(rq[:, st, :], wait).then_inc(rq_mag, 1)

            def job(self, name, jobs):
                dve, w, pp = self.dve, work[:, jobs.slot(), :], self.pp
                j = int(name[2:]) if name[2:] else 0
                kind = name[:2]
                free = slot_free[jobs.slot()]
                if kind == "XA":
                    wb = w[:, 0:512].bitcast(BF16).rearrange("p (n s) -> p n s", s=S)
                    dve.wait_ge(xq_hi_done, (self.b + 1) * 2 + (j + 1))
                    for i in range(4):
                        n = j * 4 + i
                        last = nc.vector.scalar_tensor_tensor(
                            out=xq_lo[:, n // CK, n % CK, :], in0=wb[:, i, :], scalar=col("in_scale", n),
                            in1=xq_hi[:, n // CK, n % CK, :], op0=ALU.mult, op1=ALU.subtract)
                    last.then_inc(free, 1)
                elif kind == "SP":
                    dve.wait_ge(vself_hi_done, self.pr * ST + j + 1)
                    nc.vector.scalar_tensor_tensor(out=v_lo[:, pp, j, :], in0=w[:, 3 * D:4 * D], scalar=col("wv_s"),
                                                   in1=v_hi[:, pp, j, 0:D], op0=ALU.mult, op1=ALU.subtract).then_inc(free, 1)
                    for i, c in enumerate((0, 1, 2, 4, 5)):
                        last = nc.vector.bn_stats(stats[:, j * 5 + i, :], raw_self[:, j, c * P:(c + 1) * P])
                elif kind == "KV":
                    t0, n = KV_TILES[j]
                    r = rows_of(t0)
                    dve.wait_ge(kv_evac, self.pr * len(KV_TILES) + (j + 1))
                    o = w[0:r, 0:n * 2 * D].rearrange("p (t n) -> p t n", n=2 * D)
                    nc.vector.tensor_tensor(v_lo[0:r, pp, ST + t0:ST + t0 + n, :], o[:, :, D:2 * D],
                                            v_hi[0:r, pp, ST + t0:ST + t0 + n, 0:D], ALU.subtract).then_inc(free, 1)
                    for t in range(t0, t0 + n):
                        last = nc.vector.bn_stats(stats[0:r, 10 + t, :], raw_k[0:r, t, :])
                    if j == len(KV_TILES) - 1:
                        for _ in self.norms(last, 1):
                            pass
                    if t0 + n == KT_TILES[0][1]:
                        self.chain = self.norm_self(last)
                    if j in NORM_JOBS:
                        for _ in range(8):
                            next(self.chain, None)
                elif kind == "ST":
                    dve.wait_ge(*released(jobs))
                    tokens = slice(j * P, (j + 1) * P)
                    nc.vector.tensor_copy(selfT_hi[:, pp, :, tokens], selfT_f[:, :, tokens]).then_inc(selfT_hi_done, 1)
                    dve.wait_ge(selfT_hi_done, self.pr * ST + j + 1)
                    nc.vector.tensor_tensor(selfT_lo[:, pp, :, tokens], selfT_f[:, :, tokens], selfT_hi[:, pp, :, tokens],
                                            ALU.subtract).then_inc(selfT_lo_done, 1)
                elif kind == "KT":
                    dve.wait_ge(*released(jobs))
                    c0 = KT_TILES[j][0] * P
                    n = min(SC - c0, KT_TILES[j][1] * P)
                    nc.vector.tensor_copy(kxT_hi[:, pp, c0:c0 + n], kxT_f[:, c0:c0 + n]).then_inc(kxT_hi_done, 1)
                    if j == 1:
                        dve.wait_ge(kxT_hi_done, self.pr * 2 + 2)
                        nc.vector.tensor_tensor(kxT_lo[:, pp, c0:c0 + n], kxT_f[:, c0:c0 + n], kxT_hi[:, pp, c0:c0 + n],
                                                ALU.subtract).then_inc(kxT_lo_done, 1)
                elif kind == "MX":
                    dve.wait_ge(work_ready, jobs.ready())
                    spans = w.rearrange("p (i n) -> p i n", n=512)[:, :, 0:MX_W]
                    nc.vector.tensor_reduce(mx[:, j % 2, 4 + j // 2:5 + j // 2], spans, AX_XY, ALU.max).then_inc(free, 1)
                    if j == 7:
                        self.maxima(jobs)
                elif kind == "MS":
                    dve.wait_ge(work_ready, jobs.ready())
                    nc.vector.tensor_reduce(mx[:, 0, 2 * j:2 * j + ST], w[:, 0:ST * S].rearrange("p (t n) -> p t n", n=S),
                                            AX_X, ALU.max).then_inc(free, 1)
                    if j == 1:
                        dve.wait_ge(*released(jobs))
                        nc.vector.tensor_scalar(mx_neg[:, 0:4], mx[:, 0, 0:4], -1.0, None, ALU.mult).then_inc(mx_step, 1)
                elif kind == "PJ":
                    dve.wait_ge(work_ready, jobs.ready())
                    if j == 0:
                        dve.wait_ge(xres_loaded, self.pj * 16 + 16)
                    nc.vector.scalar_tensor_tensor(out=x_res[:, j, :], in0=w[:, 0:H], scalar=col("coef"), in1=x_res[:, j, :],
                                                   op0=ALU.mult, op1=ALU.add).then_inc(free, 1)
                jobs.step()

            def norms(self, last, half):
                lo, hi = ((0, 10 + KT_TILES[0][1]), (10 + KT_TILES[0][1], 10 + CT))[half]
                dve, base = self.dve, self.pr * STAT_STEPS + half * (STAT_STEPS // 2)
                n = [0]

                def wait(ins):
                    n[0] += 1
                    ins.then_inc(stat_step, 1)
                    dve.wait_ge(stat_step, base + n[0])
                wait(last)
                yield
                yield from moments(nc, stats[:, lo:hi], D, mean[:, lo:hi], rstd[:, lo:hi],
                                   [x[:, lo:hi] for x in (st_a, st_b, st_c, st_d)], eps_w[:, lo:hi], wait)
                assert n[0] * 2 == STAT_STEPS

            def norm_self(self, last):
                yield from self.norms(last, 0)
                nc.vector.scalar_tensor_tensor(out=norm_bias[:], in0=mean[:, 5:10], scalar=-1.0, in1=rstd[:, 5:10],
                                               op0=ALU.mult, op1=ALU.mult).then_inc(norm_bias_done, 1)
                for i, c in enumerate((0, 1, 2, 4, 5)):
                    o = raw_self[:, 0, c * P:(c + 1) * P]
                    ins = nc.vector.tensor_scalar(o, o, mean[:, i:i + 1], rstd[:, i:i + 1], ALU.subtract, ALU.mult)
                ins.then_inc(self_norm[0], 1)
                yield

            def maxima(self, jobs):
                dve = self.dve
                dve.wait_ge(*released(jobs))
                nc.vector.tensor_tensor(mx[:, 0, 4:8], mx[:, 0, 4:8], mx[:, 1, 4:8], ALU.max).then_inc(mx_done, 1)
                dve.wait_ge(mx_done, self.pr + 1)
                nc.vector.tensor_scalar(mx_neg[:, 4:8], mx[:, 0, 4:8], -1.0, None, ALU.mult).then_inc(mx_step, 1)

            def low(self, k, ahead=0):
                r = P if k < ST else rows_of(k - ST)
                self.dve.wait_ge(exp_done, (self.pr if ahead else self.at) * NT + (k + 1 + EXP_CREDIT))
                nc.vector.tensor_tensor(p_lo[0:r, k % RING, :], p_f[0:r, k % RING, :], p_hi[0:r, k % RING, :], ALU.subtract)\
                    .then_inc(plo_dve, 1)

            def take_outputs(self, src, g):
                dve, a_ = self.dve, self.at
                dve.wait_ge(p_free, a_ * NT + (RING + (ST if src == 0 else NT)))
                if src == 0:
                    dve.wait_ge(smooth_loaded[self.ap], self.pair * 16 + 16)
                nc.vector.reciprocal(o_rinv[:, src, 0:3], o_ps[:, 0, D:3 * VW:VW])
                nc.vector.reciprocal(o_rinv[:, src, 3:4], o_ps[:, 1, D:D + 1]).then_inc(o_recip, 1)
                dve.wait_ge(o_recip, a_ * 2 + (src + 1))
                for j in range(4):
                    last = nc.vector.scalar_tensor_tensor(
                        out=yo[:, (src * 4 + j) * P:(src * 4 + j + 1) * P], in0=o_ps[:, j // 3, (j % 3) * VW:(j % 3) * VW + D],
                        scalar=o_rinv[:, src, j:j + 1], in1=smooth[:, self.ap, (src * 2 + j // 2) * D:(src * 2 + j // 2 + 1) * D],
                        op0=ALU.mult, op1=ALU.mult)
                last.then_inc(o_free, 1)

            def round_outputs(self, a_):
                dve, base, n = self.dve, a_ * Q_STEPS, [0]
                dve.wait_ge(o_free, a_ * 2 + 3)

                def wait(ins):
                    n[0] += 1
                    ins.then_inc(q_step, 1)
                    dve.wait_ge(q_step, base + n[0])
                self.magnitudes(yo[:], wait).then_inc(ro_mag, 1)
                assert n[0] == Q_STEPS

            def split_ctx(self, c):
                self.dve.wait_ge(ctx_hi_done, self.b * CK + (CK + c + 1))
                nc.vector.tensor_tensor(ctx_lo[:, c, :], ctx_in[:], ctx_hi[:, c, :], ALU.subtract).then_inc(ctx_split, 1)

            def body(self, b, g, jobs, attend=True, prep=True, ot=True, phase_a=False, new_row=False, pj=False, parity=None, pair=None):
                self.index(b, g, parity, pair)
                self.pj = b - 1
                normed = not attend or (isinstance(g, int) and g == 1 and not (isinstance(b, int) and b == B - 1))
                tokens = self.norm_tokens() if normed else iter(())
                steps = order(body_jobs(attend, prep, ot, phase_a, pj), attend, phase_a)
                if not attend:
                    for _ in tokens:
                        pass
                    for st in range(ST):
                        self.token_magnitudes(st)
                    for c in range(CK):
                        self.split_ctx(c)
                for k, names in enumerate(steps):
                    if attend:
                        if k % 2 == 1:
                            self.low(k + 1)
                        if prep and k + 1 == NT:
                            self.low(0, 1)
                        if k == ST:
                            if ot:
                                self.dve.wait_ge(ro_sum, self.at)
                            self.take_outputs(0, g)
                    for name in names:
                        self.job(name, jobs)
                    if k == 0 and attend and ot:
                        self.round_outputs((b - 1) * G + (G - 1) if pj else b * G + (g - 1))
                    if attend and k >= 5:
                        next(tokens, None)
                    if attend and phase_a and k in MAG_STEPS:
                        self.token_magnitudes(MAG_STEPS.index(k))
                    if attend and phase_a and k in CTX_LO_STEPS:
                        self.split_ctx(CTX_LO_STEPS.index(k))
                if attend:
                    assert next(tokens, None) is None
                    self.take_outputs(1, g)
                else:
                    self.low(0, 1)

            def tail(self, b, jobs):
                self.pj = b
                self.round_outputs(b * G + (G - 1))
                jobs.step()
                self.job("PJ0", jobs)
                self.job("PJ1", jobs)

        ROUND_STEPS = {4: (0,), 8: (1,), 10: (2,), 11: (3,)}
        NORM_TILES = {4: KT_TILES[0], 6: KT_TILES[1]}

        class Pool(Body):
            def __init__(self, pool):
                self.pool = pool

            def round_sum(self, y, n, ready, done):
                self.pool.wait_ge(ready, n + 1)
                nc.gpsimd.tensor_tensor(q_sum[:], y, q_mag[:], ALU.add).then_inc(done, 1)

            def round_difference(self, dst, n, summed, done):
                self.pool.wait_ge(summed, n + 1)
                nc.gpsimd.tensor_tensor(dst, q_sum[:], q_mag[:], ALU.subtract).then_inc(done, 1)

            def round_tokens(self, st, step):
                n = (self.b + 1) * ST + st
                if step == 0:
                    self.round_sum(rq[:, st, :], n, rq_mag, rq_sum)
                else:
                    self.round_difference(rq[:, st, :], n, rq_sum, rq_done)

            def body(self, b, g, jobs, attend=True, prep=True, ot=True, phase_a=False, new_row=False, pj=False, parity=None, pair=None):
                pool = self.pool
                self.index(b, g, parity, pair)
                steps = order(body_jobs(attend, prep, ot, phase_a, pj), attend, phase_a)
                if not attend:
                    for n in range(2 * ST):
                        self.round_tokens(n // 2, n % 2)
                for k, names in enumerate(steps):
                    if attend and k % 2 == 0 and k + 1 < NT:
                        m = k + 1
                        r = P if m < ST else rows_of(m - ST)
                        pool.wait_ge(exp_done, self.at * NT + (m + 1 + EXP_CREDIT))
                        nc.gpsimd.tensor_tensor(p_lo[0:r, m % RING, :], p_f[0:r, m % RING, :], p_hi[0:r, m % RING, :],
                                                ALU.subtract).then_inc(plo_pool, 1)
                    if prep and k in NORM_TILES:
                        t0, t1 = NORM_TILES[k][0], sum(NORM_TILES[k])
                        half = int(t0 > 0)
                        pool.wait_ge(stat_step, self.pr * STAT_STEPS + (half + 1) * (STAT_STEPS // 2))
                        r = P
                        o = raw_k[0:r, t0:t1, :]
                        nc.gpsimd.tensor_tensor(o, o, rstd[0:r, 10 + t0:10 + t1].unsqueeze(2).to_broadcast([r, t1 - t0, D]),
                                                ALU.mult).then_inc(k_norm, 1)
                    if attend and ot and k == 1:
                        self.round_sum(yo[:], self.at - 1, ro_mag, ro_sum)
                    if attend and ot and k == 2:
                        self.round_difference(ro[:], self.at - 1, ro_sum, ro_done)
                    if attend and phase_a and k in ROUND_STEPS:
                        for n in ROUND_STEPS[k]:
                            self.round_tokens(n // 2, n % 2)
                    for name in names:
                        if name == "KT0":
                            n = KT_TILES[0][1] * P
                            pool.wait_ge(kxT_hi_done, self.pr * 2 + 1)
                            nc.gpsimd.tensor_tensor(kxT_lo[:, self.pp, 0:n], kxT_f[:, 0:n],
                                                    kxT_hi[:, self.pp, 0:n], ALU.subtract).then_inc(kxT_lo_done, 1)
                        jobs.step()

            def tail(self, b, jobs):
                n = b * G + (G - 1)
                self.round_sum(yo[:], n, ro_mag, ro_sum)
                self.round_difference(ro[:], n, ro_sum, ro_done)

        class SP(Body):
            def __init__(self, sp):
                self.sp = sp

            def load_chunk(self, row, c):
                self.sp.dma_start(ctx_in[:], a["ctxT"][bass.ds(row, 1), c * P:(c + 1) * P, :].rearrange("a p n -> p (a n)"))\
                    .then_inc(ctx_loaded, 16)

            def load_tokens(self, row, to, done):
                self.sp.dma_start(to[:], a["x"][bass.ds(row, 1)].rearrange("a (t p) n -> p (a t) n", p=P)).then_inc(done, 16)

            def body(self, b, g, jobs, attend=True, prep=True, ot=True, phase_a=False, new_row=False, pj=False, parity=None, pair=None):
                sp = self.sp
                self.index(b, g, parity, pair)
                if not attend:
                    sp.wait_ge(init_done, 2)
                    self.load_tokens(0, xt, x_loaded)
                    self.load_chunk(0, 0)
                    sp.wait_ge(ctx_split, 1)
                    self.load_chunk(0, 1)
                if isinstance(g, int) and g == 1 and not (isinstance(b, int) and b == B - 1):
                    sp.wait_ge(x_step, (b + 1) * X_STEPS)
                    self.load_tokens(b + 1, xt, x_loaded)
                    sp.wait_ge(ctx_split, (b + 1) * CK)
                    self.load_chunk(b + 1, 0)
                if phase_a and attend:
                    sp.wait_ge(ctx_split, (b + 1) * CK + 1)
                    self.load_chunk(b + 1, 1)
                if prep:
                    gp = 0 if new_row else g + 1
                    if attend:
                        sp.wait_ge(o_free, self.at * 2 + 1)
                    sp.dma_start(smooth[:, self.pp, :], inv_smooth[bass.ds(gp, 1), :].partition_broadcast(P).rearrange("p a n -> p (a n)"))\
                        .then_inc(smooth_loaded[self.pp], 16)
                if pj:
                    names = sum(body_jobs(attend, prep, ot, phase_a, pj), [])
                    self.residual(b - 1, Jobs(jobs.half, jobs.const + names.index("PJ1")))

            def residual(self, row, pj1):
                sp = self.sp
                sp.wait_ge(x1_stored, row * 16 + 16)
                self.load_tokens(row, x_res, xres_loaded)
                sp.wait_ge(*released(pj1))
                sp.dma_start(x1_dram[bass.ds(row, 1)].rearrange("a (t p) n -> p (a t) n", p=P), x_res[:]).then_inc(x1_stored, 16)

            def tail(self, b, jobs):
                self.residual(b, Jobs(jobs.half, jobs.const + 2))

        with nc.Block() as block:
            @block.sync
            def _(sp):
                plan(SP(sp), sp.Fori)
                sp.wait_ge(x1_stored, 16 * B + 16)

            @block.tensor
            def _(pe):
                pe.wait_ge(init_done, 2)
                plan(PE(pe), pe.Fori)

            @block.scalar
            def _(act):
                act.wait_ge(init_done, 2)
                plan(ACTE(act), act.Fori)

            @block.vector
            def _(dve):
                nc.vector.memset(v_hi[:], 1.0).then_inc(exp_done, EXP_CREDIT)
                nc.vector.memset(v_lo[:], 0.0).then_inc(p_free, RING)
                nc.vector.memset(stats[:], 0.0).then_inc(init_done, 1)
                nc.vector.memset(eps_x[:], EPS).then_inc(o_free, 1)
                nc.vector.memset(x_mean[:], 0.0).then_inc(x1_stored, 16)
                nc.vector.memset(q_sum[:, 0:1], 0.0).then_inc(selfT_lo_done, 1)
                nc.vector.memset(q_mag[:, 0:1], 0.0).then_inc(kxT_lo_done, 1)
                nc.vector.memset(raw_k[:], 0.0).then_inc(init_done, 1)
                dve.wait_ge(init_done, 2)
                plan(DVE(dve), dve.Fori)

            @block.gpsimd
            def _(pool):
                plan(Pool(pool), pool.Fori)


TG = 4
NG = B * ST // TG
TOK = TG * P
U = E + 1
CHUNKS = U * FC


def experts_block(nc, a, x1, out):
    with ExitStack() as ctx:
        def sb(name, shape, dt):
            return ctx.enter_context(nc.sbuf_tensor(name, shape, dt))

        def sem(name):
            return ctx.enter_context(nc.semaphore(name))

        ident = sb("e_ident", [P, P], F32)
        gu_hi = sb("gu_hi", [P, CK, U * 2 * I], F16)
        gu_lo = sb("gu_lo", [P, CK, U * 2 * I], F16)
        dn_hi = sb("dn_hi", [P, FC, U * H], F16)
        dn_lo = sb("dn_lo", [P, FC, U * H], F16)
        router = sb("router", [P, CK, E], F32)
        gate = sb("gate", [P, 2], F32)
        order = sb("order", [P, TG, E], F32)
        w_loaded = [sem(f"ew{i}_loaded") for i in range(3)]
        w_hi = sem("ew_hi")
        w_lo = sem("ew_lo")
        small_loaded = sem("e_small_loaded")
        ident_step = sem("e_ident_step")

        WP, WC = 3, 1024
        AHEAD = 2
        stage = sb("e_stage", [P, WP, WC], F32)

        def staged(i):
            return stage[:, i, :] if i < CK else stage[:, i, :].rearrange("p (c n) -> p c n", c=FC)

        def load_part(sp, u, i):
            if i < CK:
                src = a["w_gu"][bass.ds(u, 1), i * P:(i + 1) * P, :].rearrange("a p n -> p (a n)")
            else:
                src = a["w_dn"][bass.ds(u, 1)].rearrange("a (c p) n -> p (a c) n", p=P)
            sp.dma_start(staged(i), src).then_inc(w_loaded[i], 16)

        def part(u, i):
            if i < CK:
                return tuple(w[:, i, bass.ds(u * (2 * I), 2 * I)] for w in (gu_hi, gu_lo))
            return tuple(w[:, :, bass.ds(u * H, H)] for w in (dn_hi, dn_lo))

        def split_hi(act, u, i):
            act.wait_ge(w_loaded[i], u * 16 + 16)
            nc.scalar.activation(part(u, i)[0], staged(i), ACT.Copy).then_inc(w_hi, 1)

        def split_lo(engine, ops, u, i):
            engine.wait_ge(w_hi, u * WP + (i + 1))
            hi, lo = part(u, i)
            ops.tensor_tensor(lo, staged(i), hi, ALU.subtract).then_inc(w_lo, 1)

        with nc.Block() as block:
            @block.sync
            def _(sp):
                for u in range(AHEAD):
                    for i in range(WP):
                        if u >= 1:
                            sp.wait_ge(w_lo, (u - 1) * WP + i + 1)
                        load_part(sp, u, i)
                sp.dma_start(router[:], a["router"].rearrange("(c p) e -> p c e", p=P)).then_inc(small_loaded, 16)
                sp.dma_start(gate[:, 0:1], a["g_ffn"].partition_broadcast(P)).then_inc(small_loaded, 16)

            @block.scalar
            def _(act):
                for u in range(AHEAD):
                    for i in range(WP):
                        split_hi(act, u, i)
                act.wait_ge(small_loaded, 32)
                nc.scalar.activation(gate[:, 1:2], gate[:, 0:1], ACT.Tanh)

            @block.vector
            def _(dve):
                for e in range(E):
                    nc.vector.memset(order[:, :, e:e + 1], float(e - E))
                for u in range(AHEAD):
                    for i in range(WP):
                        split_lo(dve, nc.vector, u, i)

            @block.gpsimd
            def _(pool):
                nc.gpsimd.memset(ident[:], 0.0).then_inc(ident_step, 1)
                pool.wait_ge(ident_step, 1)
                nc.gpsimd.affine_select(out=ident[:], in_=ident[:], compare_op=ALU.not_equal, fill=1.0, base=0,
                                        pattern=[[-1, P]], channel_multiplier=1)

        xs = sb("e_x", [P, 2, TG, H], F32)
        xn = sb("e_xn", [P, TG, H], F32)
        xr = sb("e_xr", [P, TG, H], F32)
        xT_f = sb("e_xT_f", [P, CK, TOK], F32)
        xT_hi = sb("e_xT_hi", [P, 2, CK, TOK], F16)
        xT_lo = sb("e_xT_lo", [P, 2, CK, TOK], F16)
        silu = sb("e_silu", [P, 2, TOK], F32)
        h_f = sb("e_h_f", [P, 2, TOK], F32)
        h_hi = sb("e_h_hi", [P, 2, TOK], F16)
        h_lo = sb("e_h_lo", [P, 2, TOK], F16)
        y = sb("e_y", [P, TG, H], F32)
        stats = sb("e_stats", [P, TG, 6], F32)
        mean = sb("e_mean", [P, TG], F32)
        rstd = sb("e_rstd", [P, TG], F32)
        tmp = sb("e_tmp", [P, 4, TG], F32)
        eps = sb("e_eps", [P, TG], F32)
        top = sb("e_top", [P, TG], F32)
        unused = sb("e_unused", [P, 2], F32)
        first = sb("e_first", [P, TG], F32)
        sig = sb("e_sig", [P, TG], F32)
        cand = sb("e_cand", [P, TG, E], F32)
        score = sb("e_score", [P, TG, E], F32)
        gu = ctx.enter_context(nc.psum_tensor("gu", [P, 2, 2, TOK], F32))
        acc = ctx.enter_context(nc.psum_tensor("acc", [P, TG, H], F32))
        turn = ctx.enter_context(nc.psum_tensor("turn", [P, CK, TOK], F32))

        x_loaded = [sem("e_x0_loaded"), sem("e_x1_loaded")]
        stored = sem("e_stored")
        norm_step = sem("e_norm_step")
        turned = sem("e_turned")
        xT_hi_done = sem("e_xT_hi_done")
        xT_done = sem("e_xT_done")
        logits_done = sem("e_logits_done")
        route_step = sem("e_route_step")
        sig_done = sem("e_sig_done")
        xr_done = sem("e_xr_done")
        gu_done = sem("e_gu_done")
        silu_done = sem("e_silu_done")
        h_made = sem("e_h_made")
        h_hi_done = sem("e_h_hi_done")
        h_split = sem("e_h_split")
        down_done = sem("e_down_done")
        acc_full = sem("e_acc_full")
        acc_taken = sem("e_acc_taken")
        CREDIT = 2
        NORM_STEPS = 1 + MOMENT_STEPS + 1
        ROUTE_STEPS = 7

        def groups(fori, group):
            group(0)
            with fori(1, NG) as r:
                group(r)

        def splits(r, u, c):
            return isinstance(r, int) and c < WP and not (isinstance(u, int) and u + AHEAD > E)

        def experts(fori, chunk):
            for c in range(FC):
                chunk(0, 0, c, False)
            with fori(0, E // 2 - 1) as i:
                for p in (1, 2):
                    for c in range(FC):
                        chunk(i * 2 + p, p % 2, c, False)
            for u in (E - 1, E):
                for c in range(FC):
                    chunk(u, u % 2, c, u == E)

        with nc.Block() as block:
            @block.sync
            def _(sp):
                def load(r, buf):
                    sp.dma_start(xs[:, buf], x1[bass.ds(r * (TG // ST), TG // ST)].rearrange("b (t p) n -> p (b t) n", p=P))\
                        .then_inc(x_loaded[buf], 16)

                load(0, 0)
                with sp.Fori(AHEAD, U) as u:
                    for i in range(WP):
                        sp.wait_ge(w_lo, (u - 1) * WP + (i + 1))
                        load_part(sp, u, i)
                for r in range(NG):
                    if r + 1 < NG:
                        if r >= 1:
                            sp.wait_ge(acc_taken, r + 1)
                        load(r + 1, (r + 1) % 2)
                    sp.wait_ge(acc_taken, r + 2)
                    sp.dma_start(out[bass.ds(r * (TG // ST), TG // ST)].rearrange("b (t p) n -> p (b t) n", p=P), y[:])\
                        .then_inc(stored, 16)
                sp.wait_ge(stored, 16 * NG + 16)

            @block.tensor
            def _(pe):
                def gate_up(r, u, parity, c):
                    q = r * CHUNKS + u * FC + c
                    if c == 0:
                        pe.wait_ge(xT_done, r * U + u + 2)
                        if isinstance(r, int):
                            pe.wait_ge(w_lo, u * WP + WP)
                    pe.wait_ge(h_made, q + (CREDIT - 1))
                    for half in range(2):
                        for i in range(3 * CK):
                            k, part = i // 3, i % 3
                            last = nc.tensor.matmul(
                                gu[:, c % 2, half, :],
                                (gu_hi, gu_lo, gu_hi)[part][:, k, bass.ds(u * (2 * I) + (half * I + c * P), P)],
                                (xT_hi, xT_hi, xT_lo)[part][:, parity, k, :], start=(i == 0), stop=(i == 3 * CK - 1))
                    last.then_inc(gu_done, 1)

                def turn_inputs(r, u, src):
                    pe.wait_ge(xT_done, r * U + u + 1)
                    for t in range(TG):
                        for k in range(CK):
                            last = nc.tensor.transpose(turn[:, k, t * P:(t + 1) * P], src[:, t, k * P:(k + 1) * P], ident[:])
                    last.then_inc(turned, 1)

                def down(r, u, c, final):
                    q = r * CHUNKS + u * FC + c
                    pe.wait_ge(h_split, q + (1 + CREDIT))
                    begin = isinstance(u, int) and u == 0 and c == 0
                    if begin:
                        pe.wait_ge(acc_taken, r + 1)
                    for t in range(TG):
                        for i in range(3):
                            last = nc.tensor.matmul(acc[:, t, :], (h_hi, h_hi, h_lo)[i][:, c % 2, t * P:(t + 1) * P],
                                                    (dn_hi, dn_lo, dn_hi)[i][:, c, bass.ds(u * H, H)],
                                                    start=(begin and i == 0 and t % 2 == 0),
                                                    stop=(final and c == FC - 1 and i == 2), skip_group_check=True)
                    last.then_inc(down_done, 1)

                def group(r):
                    pe.wait_ge(norm_step, r * NORM_STEPS + NORM_STEPS)
                    turn_inputs(r, 0, xn)
                    pe.wait_ge(xT_done, r * U + 2)
                    for t in range(TG):
                        for k in range(CK):
                            last = nc.tensor.matmul(turn[:, 0, t * E:(t + 1) * E], xT_f[:, k, t * P:(t + 1) * P], router[:, k, :],
                                                    start=(k == 0), stop=(k == CK - 1))
                    last.then_inc(logits_done, 1)
                    gate_up(r, 0, 0, 0)
                    gate_up(r, 0, 0, 1)

                    def chunk(u, parity, c, final):
                        if c < FC - 2:
                            gate_up(r, u, parity, c + 2)
                        elif not final:
                            gate_up(r, u + 1, 1 - parity, c + 2 - FC)
                        if c == 0 and not final:
                            pe.wait_ge(xr_done, r * E + u + 1)
                            turn_inputs(r, u + 1, xr)
                        down(r, u, c, final)
                    experts(pe.Fori, chunk)
                    nc.tensor.matmul(turn[0:1, 1, 0:1], ident[:, 0:1], ident[:, 0:1], start=True, stop=True).then_inc(acc_full, 1)

                groups(pe.Fori, group)

            @block.scalar
            def _(act):
                def turned_hi(r, u, parity, keep):
                    act.wait_ge(turned, r * U + u + 1)
                    if keep:
                        nc.scalar.activation(xT_f[:], turn[:], ACT.Copy)
                    nc.scalar.activation(xT_hi[:, parity], turn[:], ACT.Copy).then_inc(xT_hi_done, 1)

                def gate_silu(r, u, c):
                    q = r * CHUNKS + u * FC + c
                    act.wait_ge(gu_done, q + 1)
                    act.wait_ge(h_made, q + (CREDIT - 1))
                    nc.scalar.activation(silu[:, c % 2, :], gu[:, c % 2, 0, :], ACT.Silu).then_inc(silu_done, 1)

                def group(r):
                    turned_hi(r, 0, 0, True)
                    act.wait_ge(route_step, r * ROUTE_STEPS + 1)
                    nc.scalar.activation(sig[:], top[:], ACT.Tanh, scale=0.5).then_inc(sig_done, 1)
                    gate_silu(r, 0, 0)

                    def chunk(u, parity, c, final):
                        q = r * CHUNKS + u * FC + c
                        act.wait_ge(h_made, q + (1 + CREDIT))
                        act.wait_ge(down_done, q + 1)
                        nc.scalar.activation(h_hi[:, c % 2, :], h_f[:, c % 2, :], ACT.Copy).then_inc(h_hi_done, 1)
                        if c < FC - 1:
                            gate_silu(r, u, c + 1)
                        elif not final:
                            gate_silu(r, u + 1, 0)
                        if c == 0 and not final:
                            turned_hi(r, u + 1, 1 - parity, False)
                        if splits(r, u, c):
                            split_hi(act, u + AHEAD, c)
                    experts(act.Fori, chunk)

                groups(act.Fori, group)

            @block.vector
            def _(dve):
                def turned_lo(r, u, parity):
                    dve.wait_ge(xT_hi_done, r * U + u + 1)
                    nc.vector.tensor_tensor(xT_lo[:, parity], turn[:], xT_hi[:, parity], ALU.subtract).then_inc(xT_done, 1)

                def scaled(r, u):
                    dve.wait_ge(turned, r * U + u)
                    s = score[:, :, bass.ds(u - 1, 1)].to_broadcast([P, TG, H])
                    nc.vector.tensor_tensor(xr[:], xn[:], s, ALU.mult).then_inc(xr_done, 1)

                nc.vector.memset(eps[:], EPS).then_inc(h_made, CREDIT)
                nc.vector.memset(top[:], 0.0).then_inc(xT_done, 1)
                nc.vector.memset(first[:], 0.0).then_inc(acc_taken, 1)
                nc.vector.memset(rstd[:], 0.0).then_inc(stored, 16)
                def group(r2, buf):
                    r = r2 * 2 + buf
                    dve.wait_ge(x_loaded[buf], r2 * 16 + 16)
                    n = [0]

                    def wait(ins):
                        n[0] += 1
                        ins.then_inc(norm_step, 1)
                        dve.wait_ge(norm_step, r * NORM_STEPS + n[0])
                    for t in range(TG):
                        last = nc.vector.bn_stats(stats[:, t, :], xs[:, buf, t, :])
                    wait(last)
                    for _ in moments(nc, stats[:], H, mean[:], rstd[:], [tmp[:, i] for i in range(4)], eps[:], wait):
                        pass
                    for t in range(TG):
                        last = nc.vector.tensor_scalar(xn[:, t, :], xs[:, buf, t, :], mean[:, t:t + 1], rstd[:, t:t + 1],
                                                       ALU.subtract, ALU.mult)
                    wait(last)
                    assert n[0] == NORM_STEPS
                    turned_lo(r, 0, 0)

                    m = [0]

                    def route(ins):
                        m[0] += 1
                        ins.then_inc(route_step, 1)
                        dve.wait_ge(route_step, r * ROUTE_STEPS + m[0])
                    logits = turn[:, 0, 0:TG * E].rearrange("p (t e) -> p t e", e=E)
                    over_e = [P, TG, E]
                    dve.wait_ge(logits_done, r + 1)
                    route(nc.vector.tensor_reduce(top[:], logits, AX_X, ALU.max))
                    route(nc.vector.tensor_tensor(cand[:], logits, top[:].unsqueeze(2).to_broadcast(over_e), ALU.is_equal))
                    route(nc.vector.tensor_tensor(cand[:], cand[:], order[:], ALU.mult))
                    route(nc.vector.tensor_reduce(first[:], cand[:], AX_X, ALU.min))
                    route(nc.vector.tensor_tensor(cand[:], order[:], first[:].unsqueeze(2).to_broadcast(over_e), ALU.is_equal))
                    dve.wait_ge(sig_done, r + 1)
                    route(nc.vector.tensor_scalar(first[:], sig[:], 0.5, 0.5, ALU.mult, ALU.add))
                    route(nc.vector.tensor_tensor(score[:], cand[:], first[:].unsqueeze(2).to_broadcast(over_e), ALU.mult))
                    assert m[0] == ROUTE_STEPS
                    scaled(r, 1)

                    def chunk(u, parity, c, final):
                        q = r * CHUNKS + u * FC + c
                        dve.wait_ge(silu_done, q + 1)
                        dve.wait_ge(h_split, q + 1)
                        nc.vector.tensor_tensor(h_f[:, c % 2, :], silu[:, c % 2, :], gu[:, c % 2, 1, :], ALU.mult)\
                            .then_inc(h_made, 1)
                        if c == 1 and not final:
                            turned_lo(r, u + 1, 1 - parity)
                        if c == 2 and not final and not (isinstance(u, int) and u == E - 1):
                            scaled(r, u + 2)
                    experts(dve.Fori, chunk)
                    dve.wait_ge(acc_full, r + 1)
                    dve.wait_ge(stored, r * 16 + 16)
                    nc.vector.scalar_tensor_tensor(out=y[:], in0=acc[:], scalar=gate[:, 1:2], in1=xs[:, buf], op0=ALU.mult,
                                                   op1=ALU.add).then_inc(acc_taken, 1)

                for buf in range(2):
                    group(0, buf)
                with dve.Fori(1, NG // 2) as r2:
                    for buf in range(2):
                        group(r2, buf)

            @block.gpsimd
            def _(pool):
                nc.gpsimd.memset(unused[:, 0:1], 0.0).then_inc(h_split, CREDIT)
                nc.gpsimd.memset(unused[:, 1:2], 0.0).then_inc(down_done, CREDIT)
                def group(r):
                    def chunk(u, parity, c, final):
                        q = r * CHUNKS + u * FC + c
                        pool.wait_ge(h_hi_done, q + 1)
                        nc.gpsimd.tensor_tensor(h_lo[:, c % 2, :], h_f[:, c % 2, :], h_hi[:, c % 2, :], ALU.subtract)\
                            .then_inc(h_split, 1)
                        if splits(r, u, c):
                            split_lo(pool, nc.gpsimd, u + AHEAD, c)
                    experts(pool.Fori, chunk)

                groups(pool.Fori, group)


def program(nc, a, out):
    inv_smooth = nc.dram_tensor("inv_smooth", (G, 4 * D), F32, kind="Internal").ap()
    x1 = nc.dram_tensor("x1", (B, S, H), F32, kind="Internal").ap()
    attention_block(nc, a, x1, inv_smooth)
    experts_block(nc, a, x1, out)


_IN_SCALES = ["L0_xattn_q_in_scale", "L0_xattn_k_in_scale", "L0_xattn_v_in_scale", "L0_xattn_qx_in_scale"]


def kernel(**inputs):
    import numpy as np
    import concourse.bacc as bacc
    from concourse.bass_utils import run_bass_kernel_spmd

    def get(name):
        return np.asarray(inputs[name])

    def att(name):
        return get("L0_xattn_" + name)

    def group_rows(w, n):
        return w.reshape(G, n * D, H)

    arrays = {}
    arrays["x"] = get("x")
    arrays["ctxT"] = get("ctx_2048").transpose(0, 2, 1)
    arrays["w_self"] = np.concatenate([group_rows(att("wq"), HPG), group_rows(att("wk"), 1), group_rows(att("wv"), 1),
                                       group_rows(att("wqx"), HPG)], axis=1).reshape(G * GW, H).T
    kv = att("w_kv_x")
    arrays["w_kv"] = np.concatenate([group_rows(kv[:G * D], 1), group_rows(kv[G * D:], 1)], axis=1).reshape(G * 2 * D, H).T
    arrays["w_proj"] = att("wproj").T.reshape(2, G, HPG, D, H).transpose(3, 1, 0, 2, 4).reshape(D, 4 * G, H)
    arrays["smooth"] = att("proj_smooth").reshape(2, G, HPG * D).transpose(1, 0, 2).reshape(G, 4 * D)
    arrays["scales"] = np.stack([get(n) for n in _IN_SCALES])
    arrays["ln_w"], arrays["ln_b"] = att("ln_w"), att("ln_b")
    cols = [get(n).reshape(CK, P)[c] for n in _IN_SCALES for c in range(CK)]
    cols += [att(n) for n in ("qln_w", "qln_b", "kln_w", "kln_b", "qxln_w", "qxln_b", "kxln_w", "kxln_b")]
    cols += [np.broadcast_to(att(n), (P,)) for n in ("wq_scale", "wk_scale", "wqx_scale", "wv_scale", "proj_w_scale", "proj_in_scale")]
    cols += [np.broadcast_to(get("g_xattn"), (P,))]
    arrays["cols"] = np.stack(cols, axis=1)

    ffn = {n: get("L0_ffn_" + n) for n in ("router_w", "gate_up_proj", "down_proj", "shared_gate_w", "shared_up_w", "shared_down_w")}
    arrays["router"] = ffn["router_w"].T
    arrays["w_gu"] = np.concatenate([np.concatenate([ffn["shared_gate_w"], ffn["shared_up_w"]], axis=1)[None], ffn["gate_up_proj"]])
    arrays["w_dn"] = np.concatenate([ffn["shared_down_w"][None], ffn["down_proj"]])
    arrays["g_ffn"] = get("g_ffn")

    nc = bacc.Bacc("TRN2", target_bir_lowering=False, num_devices=1)
    fed, aps = {}, {}
    for name, v in arrays.items():
        v = np.ascontiguousarray(v)
        fed["in_" + name] = v
        aps[name] = nc.dram_tensor("in_" + name, v.shape, mybir.dt.from_np(v.dtype), kind="ExternalInput").ap()
    out = nc.dram_tensor("out", (B, S, H), F32, kind="ExternalOutput").ap()
    program(nc, aps, out)
    return run_bass_kernel_spmd(nc, [fed], core_ids=[0]).results[0]["out"]
```
